# Optimizing a Trainium2 kernel written in Bass

```python
import numpy as np
import jax
import jax.numpy as jnp

def _softmax(x, axis=-1):
    return jax.nn.softmax(x, axis=axis)

def _gelu(x):
    return jax.nn.gelu(x, approximate=True)

def _silu(x):
    return jax.nn.silu(x)

def _sigmoid(x):
    return jax.nn.sigmoid(x)

def _layernorm(x, axis=-1, eps=1e-05):
    m = jnp.mean(x, axis=axis, keepdims=True)
    v = jnp.var(x, axis=axis, keepdims=True)
    return (x - m) / jnp.sqrt(v + eps)

def _scatter_add(tgt, idx, src, axis=0):
    return tgt.at[idx].add(src)

def _segment_sum(src, seg, n):
    return jax.ops.segment_sum(src, seg, n)
kernel_name = 'mk_sandwich_d1_jaxref_r2_b403cd'

def setup_inputs(seed: int=0):
    np.random.seed(seed)
    _w = jnp.asarray

    def _L0_attn_setup():
        import jax, jax.numpy as jnp
        import numpy as np
        H = 16
        W = 64
        NEG = -1000000000.0

        def _neighborhood(t, nb):
            tp = jnp.pad(t, ((0, 0), (W, W), (0, 0), (0, 0)))
            idx = jnp.arange(nb)[:, None] * W + jnp.arange(3 * W)[None, :]
            return tp[:, idx]
        key = jax.random.key(seed)
        k0, k1, k2 = jax.random.split(key, 3)
        B, N, C = (2, 2048, 512)
        x = jax.random.normal(k0, (B, N, C), dtype=jnp.float32)
        w_qkv = jax.random.normal(k1, (C, 3 * C), dtype=jnp.float32) * 0.02
        w_out = jax.random.normal(k2, (C, C), dtype=jnp.float32) * 0.02
        b_out = jnp.zeros((C,), dtype=jnp.float32)
        return {'x': x, 'w_qkv': w_qkv, 'w_out': w_out, 'b_out': b_out}
    _L0_attn_in = _L0_attn_setup()

    def _L0_ffn_setup():
        import jax, jax.numpy as jnp
        import numpy as np
        B, N, D = (4, 1024, 512)
        SPARSITY = 0.01
        key = jax.random.key(seed)
        k1, k2, k3 = jax.random.split(key, 3)
        x = jax.random.normal(k1, (B, N, D), dtype=jnp.float32)
        spatial = jax.random.normal(k2, (D, D), dtype=jnp.float32) * 0.02
        freq = jnp.fft.fft(spatial, axis=-1)
        k = int(D * SPARSITY)
        mag = jnp.abs(freq)
        kth = jax.lax.top_k(mag, k)[0][:, -1:]
        w_sparse = jnp.where(mag >= kth, freq, 0.0 + 0j)
        bias = jax.random.normal(k3, (D,), dtype=jnp.float32) * 0.01
        return {'x': x, 'w_freq_real': jnp.real(w_sparse).astype(jnp.float32), 'w_freq_imag': jnp.imag(w_sparse).astype(jnp.float32), 'bias': bias}
    _L0_ffn_in = _L0_ffn_setup()
    _d = {'L0_attn_x': _L0_attn_in['x'], 'L0_attn_w_qkv': _L0_attn_in['w_qkv'], 'L0_attn_w_out': _L0_attn_in['w_out'], 'L0_attn_b_out': _L0_attn_in['b_out'], 'L0_ffn_w_freq_real': _L0_ffn_in['w_freq_real'], 'L0_ffn_w_freq_imag': _L0_ffn_in['w_freq_imag'], 'L0_ffn_bias': _L0_ffn_in['bias']}
    _x0 = _d['L0_attn_x']
    _d['L0_attn_x'] = jax.random.normal(jax.random.fold_in(jax.random.key(seed), 1), (2, 8192, 512), dtype=_x0.dtype)
    del _x0
    return _d

def reference(L0_attn_x, L0_attn_w_qkv, L0_attn_w_out, L0_attn_b_out, L0_ffn_w_freq_real, L0_ffn_w_freq_imag, L0_ffn_bias):

    def _L0_attn_ref(x, w_qkv, w_out, b_out):
        import jax, jax.numpy as jnp
        import numpy as np
        H = 16
        W = 64
        NEG = -1000000000.0

        def _neighborhood(t, nb):
            tp = jnp.pad(t, ((0, 0), (W, W), (0, 0), (0, 0)))
            idx = jnp.arange(nb)[:, None] * W + jnp.arange(3 * W)[None, :]
            return tp[:, idx]
        B, N, C = x.shape
        Dh = C // H
        scale = Dh ** (-0.5)
        pad = W // 2
        nb = N // W
        qkv = (x @ w_qkv).reshape(B, N, 3, H, Dh)
        q, k, v = (qkv[:, :, 0], qkv[:, :, 1], qkv[:, :, 2])
        qb = q.reshape(B, nb, W, H, Dh)
        kn = _neighborhood(k, nb)
        vn = _neighborhood(v, nb)
        logits = jnp.einsum('bnqhd,bnkhd->bhnqk', qb, kn) * scale
        q_idx = jnp.arange(W)[:, None]
        k_idx = jnp.arange(3 * W)[None, :]
        rel = k_idx - W - q_idx
        win = (rel >= -pad) & (rel <= pad - 1)
        j_abs = jnp.arange(nb)[:, None, None] * W + (k_idx[None] - W)
        valid = win[None] & (j_abs >= 0) & (j_abs < N)
        logits = jnp.where(valid[None, None], logits, NEG)
        attn_local = jax.nn.softmax(logits, axis=-1)
        out_local = jnp.einsum('bhnqk,bnkhd->bnqhd', attn_local, vn).reshape(B, N, H, Dh)
        kg = k[:, ::W]
        vg = v[:, ::W]
        lg = jnp.einsum('bnhd,bghd->bhng', q, kg) * scale
        attn_g = jax.nn.softmax(lg, axis=-1)
        out_global = jnp.einsum('bhng,bghd->bnhd', attn_g, vg)
        out = (out_local + out_global).reshape(B, N, C)
        return out @ w_out + b_out

    def _L0_ffn_ref(x, w_freq_real, w_freq_imag, bias):
        import jax, jax.numpy as jnp
        import numpy as np
        B, N, D = (4, 1024, 512)
        SPARSITY = 0.01
        w = jax.lax.complex(w_freq_real, w_freq_imag)
        x_freq = jnp.fft.fft(x, axis=-1)
        y_freq = jnp.einsum('bnd,do->bno', x_freq, w)
        y = jnp.real(jnp.fft.ifft(y_freq, axis=-1))
        return y + bias
    x = L0_attn_x
    x = x + _layernorm(_L0_attn_ref(_layernorm(x, axis=-1), L0_attn_w_qkv, L0_attn_w_out, L0_attn_b_out), axis=-1)
    x = x + _layernorm(_L0_ffn_ref(_layernorm(x, axis=-1), L0_ffn_w_freq_real, L0_ffn_w_freq_imag, L0_ffn_bias), axis=-1)
    return x

_drawn_inputs = setup_inputs


def setup_inputs(seed=0):
    import zlib

    import numpy as np

    out = dict(_drawn_inputs(seed))
    spreads = {'L0_attn_b_out': (0.0, 0.1)}
    factors = {'L0_ffn_bias': 8.0}
    for name, (base, spread) in spreads.items():
        noise = np.random.default_rng([zlib.crc32(name.encode()), seed]).standard_normal(out[name].shape)
        drawn = base * np.exp(spread * noise) if base else spread * noise
        out[name] = jnp.asarray(drawn.astype(out[name].dtype))
    for name, factor in factors.items():
        out[name] = (out[name] * factor).astype(out[name].dtype)
    return out
```

```python
import numpy as np
import concourse.bass as bass
from concourse import mybir
from contextlib import ExitStack

F32 = mybir.dt.float32
F32R = mybir.dt.float32r
BF16 = mybir.dt.bfloat16
ACT = mybir.ActivationFunctionType
ALU = mybir.AluOpType
AX = mybir.AxisListType

P = 128
BATCH, SEQ, D = 2, 8192, 512
HEADS, WIN = 16, 64
DH = D // HEADS
SCALE = float(DH) ** -0.5
HALF = WIN // 2
TOK = BATCH * SEQ
KT = D // P
CHUNK = 512
NCHUNK = TOK // CHUNK
CPB = SEQ // CHUNK
TILES = CHUNK // P
SPAN = CHUNK + 2 * HALF
PSEQ = SEQ + 2 * HALF
NGLOB = SEQ // WIN
GROUPS = HEADS // 4
ROWS_MAX = 3 * DH + 1
ROWS_EXP = 3 * DH + 3
NEG = -1e30
EPS = 1e-5


def masks():
    def banned(key, query):
        ok = (key - query >= 0) & (key - query <= WIN - 1)
        return np.where(ok, 0.0, NEG).astype(np.float32)
    part = np.arange(P)[:, None]
    m_max = banned(np.arange(P + WIN)[None, :], part)
    x = np.arange(256)[None, :]
    m_first = banned(part, x % P)
    m_first[:, :P] = NEG
    m_one = banned(P + part, x)
    m_mid = banned(2 * P + part, P + x)
    m_last = banned(CHUNK - HALF * 2 + part, 256 + x)
    return np.concatenate([m_max, m_first, m_one, m_mid, m_mid, m_last, m_last], axis=1)


def dft():
    n = np.arange(D)
    angle = 2.0 * np.pi * ((n[:, None] * n[None, :]) % D) / D
    c, s = np.cos(angle), np.sin(angle)
    return np.stack([c, s, c / D, -s / D]).astype(np.float32)


def project_phase(nc, x, w_qkv, q_hi_d, q_lo_d, k_hi_d, k_lo_d, v_d, kg_hi_d, kg_lo_d, bias_d, ident_d):
    NOUT = 2 * KT
    with ExitStack() as ctx:
        sb = lambda n, s, d: ctx.enter_context(nc.sbuf_tensor(n, s, d))
        sem = lambda n: ctx.enter_context(nc.semaphore(n))
        w_hi = sb("w_hi", [P, KT, 3 * D], F32R)
        w_lo = sb("w_lo", [P, KT, 3 * D], F32R)
        w_raw = sb("w_raw", [P, 2, D], F32)
        xb = [sb(f"xb{u}", [P, TILES, D], F32) for u in range(2)]
        ht_hi = [sb(f"ht_hi{u}", [P, KT, CHUNK], F32R) for u in range(2)]
        ht_lo = [sb(f"ht_lo{u}", [P, KT, CHUNK], F32R) for u in range(2)]
        o_hi = [sb(f"o_hi{u}", [P, NOUT, CHUNK], F32R) for u in range(2)]
        o_lo = [sb(f"o_lo{u}", [P, NOUT, CHUNK], F32R) for u in range(2)]
        o_v = [sb(f"o_v{u}", [P, TILES, D], F32) for u in range(2)]
        kg_hi = sb("kg_hi", [P, KT, BATCH * NGLOB], F32R)
        kg_lo = sb("kg_lo", [P, KT, BATCH * NGLOB], F32R)
        ident = sb("ident_a", [P, P], F32)
        bn = [sb(f"bn{u}", [P, TILES, 6], F32) for u in range(2)]
        mv = [sb(f"mv{u}", [P, TILES, 2], F32) for u in range(2)]
        ve = [sb(f"ve{u}", [P, TILES], F32) for u in range(2)]
        rstd = [sb(f"rstd{u}", [P, TILES], F32) for u in range(2)]
        mhalf = sb("mhalf_a", [P, TILES], F32)
        pt = [ctx.enter_context(nc.psum_tensor(f"pt{i}", [P, KT, P], F32)) for i in range(2)]
        po = [ctx.enter_context(nc.psum_tensor(f"po{i}", [P, D], F32)) for i in range(6)]
        zero = sb("zero", [P, D], F32)
        negs = sb("negs", [1, HALF], F32)

        raw_loaded = [sem(f"raw_loaded{i}") for i in range(2)]
        w_hi_done, w_lo_done = sem("w_hi_done"), sem("w_lo_done")
        ident_loaded = sem("ident_loaded")
        x_loaded = [sem(f"x_loaded{u}") for u in range(2)]
        inited = sem("inited")
        held = sem("held")
        bn_done, aggr_done = sem("bn_done"), sem("aggr_done")
        ve_done, rstd_done = sem("ve_done"), sem("rstd_done")
        xn_done = sem("xn_done")
        t_done, t_hi, t_lo = sem("t_done"), sem("t_hi"), sem("t_lo")
        mm_done, ev_act, ev_dve = sem("mm_done"), sem("ev_act"), sem("ev_dve")
        stored = [sem(f"stored{u}") for u in range(2)]
        kg_copied, kg_stored, pads = sem("kg_copied"), sem("kg_stored"), sem("pads")

        x_v = x.rearrange("b (n p) d -> p (b n) d", p=P)

        def at_least(eng, s, per, c, off):
            if not isinstance(c, int) or per * c + off > 0:
                eng.wait_ge(s, c * per + off)

        def chunks(eng, body, first):
            first()
            for c in range(2):
                body(c, c, True)
            with eng.Fori(1, NCHUNK // 2 - 1) as pair:
                for u in range(2):
                    body(pair * 2 + u, u, True)
            body(NCHUNK - 2, 0, True)
            body(NCHUNK - 1, 1, False)

        with nc.Block() as block:
            @block.sync
            def _(sp):
                for n in range(3 * KT):
                    if n >= 2:
                        sp.wait_ge(w_hi_done, n - 1)
                        sp.wait_ge(w_lo_done, n - 1)
                    if n == 1:
                        sp.dma_start(ident[:], ident_d).then_inc(ident_loaded, 16)
                    if n == 2:
                        sp.dma_start(xb[0][:], x_v[:, 0:TILES, :]).then_inc(x_loaded[0], 16)
                    kt, part = n // 3, n % 3
                    sp.dma_start(w_raw[:, n % 2, :],
                                 w_qkv[kt * P:(kt + 1) * P, part * D:(part + 1) * D]).then_inc(raw_loaded[n % 2], 16)
                sp.wait_ge(inited, 3)
                n_pads = 0
                for b in range(BATCH):
                    for at in (b * PSEQ, b * PSEQ + HALF + SEQ):
                        for kd in (k_hi_d, k_lo_d):
                            sp.dma_start(kd[:, at:at + HALF].rearrange("(a p) n -> p a n", p=P),
                                         zero[:, 0:KT * HALF].rearrange("p (a n) -> p a n", a=KT)).then_inc(pads, 16)
                        sp.dma_start(v_d[at:at + HALF, :], zero[0:HALF, :]).then_inc(pads, 16)
                        sp.dma_start(bias_d[:, at:at + HALF], negs[:, :]).then_inc(pads, 16)
                        n_pads += 4
                    sp.dma_start(bias_d[:, b * PSEQ + HALF:b * PSEQ + HALF + SEQ].rearrange("o (p n) -> (o p) n", p=P),
                                 zero[:, 0:SEQ // P]).then_inc(pads, 16)
                    n_pads += 1

                def body(c, u, has_next):
                    if has_next:
                        at_least(sp, t_done, TILES, c, 0)
                        sp.dma_start(xb[1 - u][:], x_v[:, bass.ds((c + 1) * TILES, TILES), :]).then_inc(x_loaded[1 - u], 16)
                    sp.wait_ge(ev_act, c * (NOUT + TILES) + NOUT + TILES)
                    sp.wait_ge(ev_dve, c * NOUT + NOUT)
                    pad_at = c * CHUNK + (c // CPB) * (PSEQ - SEQ) + HALF
                    for src, qd, kd in ((o_hi[u], q_hi_d, k_hi_d), (o_lo[u], q_lo_d, k_lo_d)):
                        sp.dma_start(qd.rearrange("(a p) n -> p a n", p=P)[:, :, bass.ds(c * CHUNK, CHUNK)],
                                     src[:, 0:KT, :].bitcast(F32)).then_inc(stored[u], 16)
                        sp.dma_start(kd.rearrange("(a p) n -> p a n", p=P)[:, :, bass.ds(pad_at, CHUNK)],
                                     src[:, KT:NOUT, :].bitcast(F32)).then_inc(stored[u], 16)
                    sp.dma_start(v_d[bass.ds(pad_at, CHUNK), :].rearrange("(t p) d -> p t d", p=P),
                                 o_v[u][:]).then_inc(stored[u], 16)

                chunks(sp, body, lambda: None)
                sp.wait_ge(kg_copied, 2 * NCHUNK)
                sp.dma_start(kg_hi_d.rearrange("(a p) n -> p a n", p=P), kg_hi[:].bitcast(F32)).then_inc(kg_stored, 16)
                sp.dma_start(kg_lo_d.rearrange("(a p) n -> p a n", p=P), kg_lo[:].bitcast(F32)).then_inc(kg_stored, 16)
                sp.wait_ge(kg_stored, 32)
                sp.wait_ge(pads, 16 * n_pads)
                for u in range(2):
                    sp.wait_ge(stored[u], 16 * 5 * NCHUNK // 2)

            @block.gpsimd
            def _(pool):
                pool.memset(zero[:], 0.0).then_inc(inited, 1)
                pool.memset(negs[:], NEG).then_inc(inited, 1)
                pool.memset(mhalf[:], -0.5).then_inc(inited, 1)
                pool.wait_ge(inited, 3)

                def rstds(c, u):
                    pool.wait_ge(aggr_done, c * TILES + TILES)
                    at_least(pool, xn_done, TILES, c, -TILES)
                    pool.sem_inc(held, 1)
                    pool.tensor_scalar(ve[u][:], mv[u][:, :, 1], EPS, None, ALU.add).then_inc(ve_done, 1)
                    pool.wait_ge(ve_done, c + 1)
                    pool.tensor_tensor(rstd[u][:], ve[u][:], mhalf[:], ALU.pow).then_inc(rstd_done, 1)

                def body(c, u, has_next):
                    if has_next:
                        rstds(c + 1, 1 - u)
                    pool.wait_ge(ev_act, c * (NOUT + TILES) + NOUT)
                    pool.wait_ge(ev_dve, c * NOUT + NOUT)
                    for src, dst in ((o_hi[u], kg_hi), (o_lo[u], kg_lo)):
                        pool.tensor_copy(dst[:, :, bass.ds(c * (CHUNK // WIN), CHUNK // WIN)],
                                         src[:, KT:NOUT, ::WIN].bitcast(F32)).then_inc(kg_copied, 1)

                chunks(pool, body, lambda: rstds(0, 0))

            @block.scalar
            def _(act):
                for n in range(3 * KT):
                    kt, part = n // 3, n % 3
                    act.wait_ge(raw_loaded[n % 2], 16 * (n // 2 + 1))
                    nc.scalar.activation(w_hi[:, kt, part * D:(part + 1) * D], w_raw[:, n % 2, :], ACT.Copy).then_inc(w_hi_done, 1)

                def t_evac(c, u, t):
                    act.wait_ge(t_done, c * TILES + t + 1)
                    if t == 0:
                        at_least(act, mm_done, NOUT + TILES, c, -(NOUT + TILES))
                    nc.scalar.activation(ht_hi[u][:, :, t * P:(t + 1) * P], pt[t % 2][:], ACT.Copy).then_inc(t_hi, 1)

                def body(c, u, has_next):
                    if not isinstance(c, int) or c >= 2:
                        act.wait_ge(stored[u], (c // 2) * 80)
                        act.wait_ge(kg_copied, c * 2 - 2)
                    for o in range(NOUT + TILES):
                        act.wait_ge(mm_done, c * (NOUT + TILES) + o + 1)
                        dst = o_hi[u][:, o, :] if o < NOUT else o_v[u][:, o - NOUT, :]
                        nc.scalar.activation(dst, po[o % 6][:], ACT.Copy).then_inc(ev_act, 1)
                        if has_next and o % 3 == 2:
                            t_evac(c + 1, 1 - u, o // 3)

                chunks(act, body, lambda: [t_evac(0, 0, t) for t in range(TILES)])

            @block.vector
            def _(dve):
                for n in range(3 * KT):
                    kt, part = n // 3, n % 3
                    dve.wait_ge(w_hi_done, n + 1)
                    nc.vector.tensor_tensor(w_lo[:, kt, part * D:(part + 1) * D], w_raw[:, n % 2, :],
                                            w_hi[:, kt, part * D:(part + 1) * D].bitcast(F32), ALU.subtract).then_inc(w_lo_done, 1)

                def stats(c, u):
                    dve.wait_ge(x_loaded[u], (c // 2) * 16 + 16)
                    for t in range(TILES):
                        nc.vector.bn_stats(bn[u][:, t, :], xb[u][:, t, :]).then_inc(bn_done, 1)
                    for t in range(TILES):
                        dve.wait_ge(bn_done, c * TILES + t + 1)
                        dve.sem_inc(held, 1)
                        nc.vector.bn_aggr(mv[u][:, t, :], bn[u][:, t, :]).then_inc(aggr_done, 1)

                def norm(c, u, t):
                    if t == 0:
                        dve.wait_ge(rstd_done, c + 1)
                        dve.wait_ge(aggr_done, c * TILES + TILES)
                    nc.vector.tensor_scalar(xb[u][:, t, :], xb[u][:, t, :], mv[u][:, t, 0:1], rstd[u][:, t:t + 1],
                                            ALU.subtract, ALU.mult).then_inc(xn_done, 1)

                def t_evac(c, u, t):
                    dve.wait_ge(t_hi, c * TILES + t + 1)
                    if t == 0:
                        at_least(dve, mm_done, NOUT + TILES, c, -(NOUT + TILES))
                    nc.vector.tensor_tensor(ht_lo[u][:, :, t * P:(t + 1) * P], pt[t % 2][:],
                                            ht_hi[u][:, :, t * P:(t + 1) * P].bitcast(F32), ALU.subtract).then_inc(t_lo, 1)

                def first():
                    stats(0, 0)
                    for t in range(TILES):
                        norm(0, 0, t)
                    for t in range(TILES):
                        t_evac(0, 0, t)

                def body(c, u, has_next):
                    if has_next:
                        stats(c + 1, 1 - u)
                        for t in range(TILES):
                            norm(c + 1, 1 - u, t)
                    if not isinstance(c, int) or c >= 2:
                        dve.wait_ge(stored[u], (c // 2) * 80)
                        dve.wait_ge(kg_copied, c * 2 - 2)
                    for o in range(NOUT + TILES):
                        if o < NOUT:
                            dve.wait_ge(ev_act, c * (NOUT + TILES) + o + 1)
                            nc.vector.tensor_tensor(o_lo[u][:, o, :], po[o % 6][:], o_hi[u][:, o, :].bitcast(F32),
                                                    ALU.subtract).then_inc(ev_dve, 1)
                        if has_next and o % 3 == 2:
                            t_evac(c + 1, 1 - u, o // 3)

                chunks(dve, body, first)

            @block.tensor
            def _(pe):
                pe.wait_ge(ident_loaded, 16)

                def transposes(c, u, t):
                    pe.wait_ge(xn_done, c * TILES + t + 1)
                    at_least(pe, t_lo, TILES, c, t - 1)
                    for k in range(KT):
                        last = nc.tensor.transpose(pt[t % 2][:, k, :], xb[u][:, t, k * P:(k + 1) * P], ident[:])
                    last.then_inc(t_done, 1)

                def body(c, u, has_next):
                    pe.wait_ge(t_hi, c * TILES + TILES)
                    pe.wait_ge(t_lo, c * TILES + TILES)
                    for o in range(NOUT + TILES):
                        p = (o - 6) % (NOUT + TILES)
                        off = 0 if o >= 6 else -1
                        if p < NOUT:
                            at_least(pe, ev_dve, NOUT, c, off * NOUT + p + 1)
                        else:
                            at_least(pe, ev_act, NOUT + TILES, c, off * (NOUT + TILES) + p + 1)
                        for k in range(KT):
                            for n, (ha, wa) in enumerate(((ht_hi, w_hi), (ht_lo, w_hi), (ht_hi, w_lo))):
                                start, stop = k == 0 and n == 0, k == KT - 1 and n == 2
                                if o < NOUT:
                                    last = nc.tensor.matmul(po[o % 6][:], wa[:, k, o * P:(o + 1) * P], ha[u][:, k, :],
                                                            start=start, stop=stop)
                                else:
                                    t = o - NOUT
                                    last = nc.tensor.matmul(po[o % 6][:], ha[u][:, k, t * P:(t + 1) * P],
                                                            wa[:, k, 2 * D:3 * D], start=start, stop=stop)
                        last.then_inc(mm_done, 1)
                        if has_next and o % 3 == 1:
                            transposes(c + 1, 1 - u, o // 3)

                def first():
                    for t in range(TILES):
                        transposes(0, 0, t)
                    pe.wait_ge(w_lo_done, 3 * KT)

                chunks(pe, body, first)


def spectral_phase(nc, w_real, w_imag, dft_d, w_out, m_hi, m_lo, wo_hi, wo_lo):
    with ExitStack() as ctx:
        sb = lambda n, s, d: ctx.enter_context(nc.sbuf_tensor(n, s, d))
        sem = lambda n: ctx.enter_context(nc.semaphore(n))
        wr, wi, wo = (sb(n, [P, KT, D], F32) for n in ("wr", "wi", "wo_raw"))
        tr = [sb(f"dft{i}", [P, KT, D], F32) for i in range(4)]
        nwr = sb("nwr", [P, KT, D], F32)
        at, bt = sb("at", [P, KT, D], F32), sb("bt", [P, KT, D], F32)
        ps = [ctx.enter_context(nc.psum_tensor(f"pm{i}", [P, D], F32)) for i in range(4)]
        loaded, neg_done, mm_done, ab_done = sem("s_loaded"), sem("s_neg"), sem("s_mm"), sem("s_ab")
        hi_done, lo_done = sem("s_hi"), sem("s_lo")
        with nc.Block() as block:
            @block.sync
            def _(sp):
                for src, dst in ((w_real, wr), (w_imag, wi), (w_out, wo)):
                    sp.dma_start(dst[:], src.rearrange("(a p) n -> p a n", p=P)).then_inc(loaded, 16)
                for i in range(4):
                    sp.dma_start(tr[i][:], dft_d[i].rearrange("(a p) n -> p a n", p=P)).then_inc(loaded, 16)

            @block.tensor
            def _(pe):
                pe.wait_ge(loaded, 16 * 7)
                pe.wait_ge(neg_done, 1)
                steps = [(wr, tr[0], wi, tr[1]), (wi, tr[0], nwr, tr[1]), (at, tr[2], bt, tr[3])]
                n = 0
                for l0, r0, l1, r1 in steps:
                    if l0 is at:
                        pe.wait_ge(ab_done, 2 * KT)
                    for a in range(KT):
                        if 4 <= n < 2 * KT:
                            pe.wait_ge(ab_done, n - 3)
                        for k in range(KT):
                            nc.tensor.matmul(ps[n % 4][:], l0[:, k, a * P:(a + 1) * P], r0[:, k, :], start=k == 0, stop=False)
                            last = nc.tensor.matmul(ps[n % 4][:], l1[:, k, a * P:(a + 1) * P], r1[:, k, :], start=False, stop=k == KT - 1)
                        last.then_inc(mm_done, 1)
                        n += 1

            @block.scalar
            def _(act):
                act.wait_ge(loaded, 16 * 7)
                for k in range(KT):
                    nc.scalar.activation(wo_hi[:, k, :], wo[:, k, :], ACT.Copy).then_inc(hi_done, 1)
                for a in range(KT):
                    act.wait_ge(mm_done, 2 * KT + a + 1)
                    nc.scalar.activation(m_hi[:, a, :], ps[a][:], ACT.Copy).then_inc(hi_done, 1)

            @block.vector
            def _(dve):
                dve.wait_ge(loaded, 16 * 7)
                nc.vector.tensor_scalar(nwr[:], wr[:], -1.0, None, ALU.mult).then_inc(neg_done, 1)
                for k in range(KT):
                    dve.wait_ge(hi_done, k + 1)
                    nc.vector.tensor_tensor(wo_lo[:, k, :], wo[:, k, :], wo_hi[:, k, :].bitcast(F32), ALU.subtract).then_inc(lo_done, 1)
                for n in range(2 * KT):
                    dve.wait_ge(mm_done, n + 1)
                    nc.vector.tensor_copy((at if n < KT else bt)[:, n % KT, :], ps[n % 4][:]).then_inc(ab_done, 1)
                for a in range(KT):
                    dve.wait_ge(hi_done, KT + a + 1)
                    nc.vector.tensor_tensor(m_lo[:, a, :], ps[a][:], m_hi[:, a, :].bitcast(F32), ALU.subtract).then_inc(lo_done, 1)


def attention_phase(nc, x, b_out, b_ffn, q_hi_d, q_lo_d, k_hi_d, k_lo_d, v_d, kg_hi_d, kg_lo_d, bias_d,
                    ident_d, mask_d, m_hi, m_lo, wo_hi, wo_lo, out):
    with ExitStack() as ctx:
        sb = lambda n, s, d: ctx.enter_context(nc.sbuf_tensor(n, s, d))
        pb = lambda n, s: ctx.enter_context(nc.psum_tensor(n, s, F32))
        sem = lambda n: ctx.enter_context(nc.semaphore(n))
        MW = P + WIN
        qs = [sb(f"qs{g}", [P, 4, CHUNK], F32R) for g in range(GROUPS)]
        ks = [sb(f"ks{g}", [P, 4, SPAN], F32R) for g in range(GROUPS)]
        kgs = [sb(f"kgs{g}", [P, 4, NGLOB], F32R) for g in range(GROUPS)]
        vw = [sb(f"vw{g}", [P, 4, P], F32) for g in range(GROUPS)]
        vl = [sb(f"vl{g}", [P, P], F32) for g in range(GROUPS)]
        vg = [sb(f"vg{g}", [P, P], F32) for g in range(GROUPS)]
        p_loc = sb("p_loc", [P, 4, 4, MW], F32)
        p_last = sb("p_last", [P, 4, WIN], F32)
        p_glob = sb("p_glob", [P, 4, CHUNK], F32)
        ones = sb("ones", [P, DH], F32)
        mask = sb("mask", [P, MW + 6 * 256], BF16)
        ident = sb("ident", [P, P], F32)
        ident_b = sb("ident_b", [P, P], BF16)
        one_row = p_loc[0:1, 0, 0:3, :].rearrange("p j n -> p (j n)")
        CONST_MADE = 3 + 3 * GROUPS
        CONST_LOADS = 16 * (3 + 2 * GROUPS)
        mx = [sb(f"mx{u}", [P, TILES, 2, 4], F32) for u in range(2)]
        mt = sb("mt", [8, CHUNK], F32R)
        lns, rinv, rtmp = (sb(n, [P, CHUNK], F32) for n in ("lns", "rinv", "rtmp"))
        o_loc = sb("o_loc", [P, CHUNK], F32)
        o_glob = sb("o_glob", [P, CHUNK], F32)
        ot_hi = sb("ot_hi", [P, KT, CHUNK], F32R)
        ot_lo = sb("ot_lo", [P, KT, CHUNK], F32R)
        xb = sb("x_res", [P, TILES, D], F32)
        yb = sb("y_buf", [P, TILES, D], F32)
        th = sb("th", [P, 2, KT, P], F32R)
        tl = sb("tl", [P, 2, KT, P], F32R)
        bo = sb("bo", [P, D], F32)
        bf = sb("bf", [P, D], F32)
        bn = [sb(f"bnb{s}", [P, TILES, 6], F32) for s in range(3)]
        mv = [sb(f"mvb{s}", [P, TILES, 2], F32) for s in range(3)]
        ve = [sb(f"veb{s}", [P, TILES], F32) for s in range(3)]
        rs = [sb(f"rsb{s}", [P, TILES], F32) for s in range(3)]
        mhalf = sb("mhalf_b", [P, 1], F32)

        ps_max = pb("ps_max", [P, 2, 512])
        ps_loc = pb("ps_loc", [P, 2, 512])
        ps_glob = pb("ps_glob", [P, 512])
        ps_misc = pb("ps_misc", [P, 512])
        ps_o = pb("ps_o", [P, 512])
        ps_s = pb("ps_s", [P, 512])

        held = sem("held_b")
        mask_cast, ident_cast = sem("mask_cast"), sem("ident_cast")
        const_loaded, const_made = sem("const_loaded"), sem("const_made")
        st_loaded = [sem(f"st_loaded{g}") for g in range(GROUPS)]
        v_loaded = [sem(f"v_loaded{g}") for g in range(GROUPS)]
        m_loaded = [sem(f"m_loaded{g}") for g in range(GROUPS)]
        x_loaded = [sem(f"xr_loaded{i}") for i in range(TILES)]
        y_stored = [sem(f"y_stored{i}") for i in range(TILES)]
        max_scored, max_taken = sem("max_scored"), sem("max_taken")
        mt_done, mt_copied = sem("mt_done"), sem("mt_copied")
        loc_scored, loc_exped = sem("loc_scored"), sem("loc_exped")
        glob_scored, glob_exped = sem("glob_scored"), sem("glob_exped")
        pvl_done, pvg_done = sem("pvl_done"), sem("pvg_done")
        ln_done, inv_done = sem("ln_done"), sem("inv_done")
        nr_step = sem("nr_step")
        o_done = sem("o_done")
        o_sum = sem("o_sum")
        oth_done, otl_done = sem("oth_done"), sem("otl_done")
        out_mm, ffn_mm, tr_done = sem("out_mm"), sem("ffn_mm"), sem("tr_done")
        y_added, z_added = sem("y_added"), sem("z_added")
        th_done, tl_done = sem("th_done"), sem("tl_done")
        bn_done = [sem(f"bnb_done{s}") for s in range(3)]
        aggr_done = [sem(f"aggrb_done{s}") for s in range(3)]
        ve_done = [sem(f"veb_done{s}") for s in range(3)]
        rs_done = [sem(f"rsb_done{s}") for s in range(3)]
        nm_done = [sem(f"nmb_done{s}") for s in range(3)]
        x1_done, z_done = sem("x1_done"), sem("z_done")

        def at_least(eng, s, per, c, off):
            if not isinstance(c, int) or per * c + off > 0:
                eng.wait_ge(s, c * per + off)

        TAIL_AT = dict(out=3, y=4, x1=5, x1n=6, tr=7, ffn=8, z=9)

        def order(attend, tail, more):
            items = []
            for g in range(GROUPS):
                ahead = attend and (more or g < GROUPS - 1)
                units = iter(range(8))

                def tail_items(names):
                    if tail:
                        for name in names:
                            i = 4 * g + hh - TAIL_AT[name]
                            if 0 <= i < TILES:
                                items.append((name, g, i))

                for hh in range(4):
                    if hh == 3 and ahead:
                        items.append(("mt", g, 0))
                    if attend:
                        items.append(("loc", g, hh))
                    if ahead and hh < 3:
                        items.append(("max", g, next(units)))
                    tail_items(("z", "x1", "y", "x1n", "tr"))
                    if hh == 0:
                        tail_items(("out", "ffn"))
                        if (attend and g > 0) or (g == 0 and tail):
                            items.append(("pvg", g, 0))
                    if attend:
                        items.append(("glob", g, hh))
                    if ahead:
                        for _ in range((2, 2, 1, 0)[hh]):
                            items.append(("max", g, next(units)))
                    if hh > 0:
                        tail_items(("out", "ffn"))
                    if hh == 2 and ((attend and g > 0) or (g == 0 and tail)):
                        items.append(("ot", g, 0))
                if attend:
                    items.append(("last", g, 0))
                    items.append(("pvl", g, 0))
            return items

        def chunks(eng, item):
            for c, kind in ((0, "first"), (None, "loop"), (NCHUNK - 1, "final"), (NCHUNK, "tail")):
                attend, tail, more = kind != "tail", kind != "first", kind in ("first", "loop")
                if kind == "loop":
                    with eng.Fori(1, NCHUNK - 1) as cc:
                        for it in order(attend, tail, more):
                            item(cc, *it, more)
                else:
                    for it in order(attend, tail, more):
                        item(c, *it, more)

        def misc_users(attend, tail, more):
            users = [("mt", GROUPS - 1, 0)] + [it for it in order(attend, tail, more)
                                               if it[0] in ("mt", "out", "tr", "ffn")]
            return dict(zip(users[1:], [("mt", -1 if attend else -2, 0)] + users[1:-1]))

        with nc.Block() as block:
            @block.sync
            def _(sp):
                sp.dma_start(ident[:], ident_d).then_inc(const_loaded, 16)
                sp.dma_start(bo[:], b_out.rearrange("(o n) -> o n", o=1).to_broadcast([P, D])).then_inc(const_loaded, 16)
                sp.dma_start(bf[:], b_ffn.rearrange("(o n) -> o n", o=1).to_broadcast([P, D])).then_inc(const_loaded, 16)

                def load_stack(c, g):
                    pad_at = c * CHUNK + (c // CPB) * (PSEQ - SEQ)
                    glob_at = (c // CPB) * NGLOB
                    rows = slice(g * P, (g + 1) * P)
                    for r, (qd, kd, gd) in enumerate(((q_hi_d, k_hi_d, kg_hi_d), (q_hi_d, k_lo_d, kg_lo_d),
                                                      (q_lo_d, k_hi_d, kg_hi_d))):
                        dst = slice(r * DH, (r + 1) * DH)
                        sp.dma_start(qs[g][dst, :, :].bitcast(F32),
                                     qd[rows, :].rearrange("(h p) n -> p h n", p=DH)[:, :, bass.ds(c * CHUNK, CHUNK)]).then_inc(st_loaded[g], 16)
                        sp.dma_start(ks[g][dst, :, :].bitcast(F32),
                                     kd[rows, :].rearrange("(h p) n -> p h n", p=DH)[:, :, bass.ds(pad_at, SPAN)]).then_inc(st_loaded[g], 16)
                        sp.dma_start(kgs[g][dst, :, :].bitcast(F32),
                                     gd[rows, :].rearrange("(h p) n -> p h n", p=DH)[:, :, bass.ds(glob_at, NGLOB)]).then_inc(st_loaded[g], 16)
                    sp.dma_start(ks[g][3 * DH:ROWS_MAX, :, :].bitcast(F32),
                                 bias_d[:, bass.ds(pad_at, SPAN)].rearrange("o (a n) -> o a n", a=1).to_broadcast([1, 4, SPAN])).then_inc(st_loaded[g], 16)

                def load_values(c, g):
                    pad_at = c * CHUNK + (c // CPB) * (PSEQ - SEQ)
                    cols = slice(g * P, (g + 1) * P)
                    sp.dma_start(vw[g][:], v_d[bass.ds(pad_at, CHUNK), cols].rearrange("(t p) d -> p t d", p=P)).then_inc(v_loaded[g], 16)
                    sp.dma_start(vl[g][P - WIN:P, :], v_d[bass.ds(pad_at + CHUNK, WIN), cols]).then_inc(v_loaded[g], 16)
                    sp.dma_start(vg[g][:], v_d[bass.ds((c // CPB) * PSEQ + HALF, SEQ), cols]
                                 .rearrange("(t w) d -> t w d", w=WIN)[:, 0, :]).then_inc(v_loaded[g], 16)

                sp.wait_ge(const_made, CONST_MADE)
                for g in range(GROUPS):
                    load_stack(0, g)
                    load_values(0, g)

                def item(c, name, g, i, more):
                    if name == "loc" and g == 0 and i == 0:
                        if not isinstance(c, int) or c > 0:
                            for t in range(TILES):
                                at_least(sp, z_done, TILES, c, -TILES)
                                sp.dma_start(xb[:, t, :], x.rearrange("b n d -> (b n) d")[bass.ds((c - 1) * CHUNK + t * P, P), :]).then_inc(x_loaded[t], 16)
                    if name == "pvg":
                        sp.wait_ge(pvg_done, c * GROUPS + g)
                        if g > 0 and more:
                            load_values(c + 1, g - 1)
                        if g == 0 and (not isinstance(c, int) or c < NCHUNK):
                            load_values(c, GROUPS - 1)
                    if name == "last" and more:
                        sp.wait_ge(loc_scored, c * 20 + 5 * g + 5)
                        load_stack(c + 1, g)
                    if name == "z":
                        n = c * TILES + i + 1 - TILES
                        sp.wait_ge(z_done, n)
                        sp.dma_start(out.rearrange("b n d -> (b n) d")[bass.ds((c - 1) * CHUNK + i * P, P), :],
                                     yb[:, i, :]).then_inc(y_stored[i], 16)

                for c, kind in ((0, "first"), (None, "loop"), (NCHUNK - 1, "final"), (NCHUNK, "tail")):
                    if kind == "loop":
                        with sp.Fori(1, NCHUNK - 1) as cc:
                            for it in order(True, True, True):
                                item(cc, *it, True)
                    else:
                        if kind == "tail":
                            item(c, "loc", 0, 0, False)
                        for it in order(kind != "tail", kind != "first", kind == "first"):
                            item(c, *it, kind == "first")
                for i in range(TILES):
                    sp.wait_ge(y_stored[i], 16 * NCHUNK)

            @block.gpsimd
            def _(pool):
                pool.memset(ones[:], 1.0).then_inc(const_made, 1)
                pool.memset(mhalf[:], -0.5).then_inc(const_made, 1)
                pool.dma_start(mask[:], mask_d).then_inc(mask_cast, 16)
                pool.dma_start(ident_b[:], ident_d).then_inc(ident_cast, 16)
                pool.wait_ge(const_made, 2)

                def power(c, s, i):
                    n = c * TILES + i + 1 - TILES
                    pool.wait_ge(aggr_done[s], n)
                    pool.sem_inc(held, 1)
                    pool.tensor_scalar(ve[s][:, i:i + 1], mv[s][:, i, 1:2], EPS, None, ALU.add).then_inc(ve_done[s], 1)
                    pool.wait_ge(ve_done[s], n)
                    pool.tensor_tensor(rs[s][:, i:i + 1], ve[s][:, i:i + 1], mhalf[:], ALU.pow).then_inc(rs_done[s], 1)

                def item(c, name, g, i, more):
                    n = c * TILES + i + 1 - TILES
                    if name == "out":
                        power(c, 0, i)
                    if name == "y":
                        pool.wait_ge(nm_done[0], n)
                        pool.wait_ge(x_loaded[i], c * 16)
                        pool.tensor_tensor(xb[:, i, :], xb[:, i, :], yb[:, i, :], ALU.add).then_inc(x1_done, 1)
                    if name == "x1":
                        power(c, 1, i)
                    if name == "ffn":
                        power(c, 2, i)
                    if name == "z":
                        pool.wait_ge(nm_done[2], n)
                        pool.tensor_tensor(yb[:, i, :], yb[:, i, :], xb[:, i, :], ALU.add).then_inc(z_done, 1)
                    if name == "pvg":
                        pool.wait_ge(o_done, (c * GROUPS + g) * 2)
                        at_least(pool, otl_done, GROUPS, c, g - 1)
                        pool.tensor_tensor(o_loc[:], o_loc[:], o_glob[:], ALU.add).then_inc(o_sum, 1)

                chunks(pool, item)

            @block.scalar
            def _(act):
                nc.scalar.preload_act_table_set("natural_log_exp_and_others")
                act.wait_ge(const_made, CONST_MADE)
                for g in range(GROUPS):
                    act.dma_start(ks[g][ROWS_MAX:ROWS_MAX + 1, :, :].bitcast(F32),
                                  one_row.rearrange("o (a n) -> o a n", a=1).to_broadcast([1, 4, SPAN])).then_inc(const_loaded, 16)
                    act.dma_start(kgs[g][ROWS_MAX + 1:ROWS_EXP, :, :].bitcast(F32),
                                  one_row[:, 0:4 * NGLOB]).then_inc(const_loaded, 16)

                def invert(c, off):
                    nc.scalar.activation(lns[:], ps_s[:], ACT.Ln).then_inc(ln_done, 1)
                    act.wait_ge(ln_done, c * 8 + off)
                    at_least(act, o_done, 8, c, off - 1)
                    nc.scalar.activation(rinv[:], lns[:], ACT.Exp, scale=-1.0).then_inc(inv_done, 1)

                def copy_maxima(c, g):
                    act.wait_ge(mt_done, c * GROUPS + g + 1)
                    if g > 0:
                        act.wait_ge(m_loaded[g - 1], c * 32 + 32)
                    nc.scalar.activation(mt[:], ps_misc[0:8, :], ACT.Copy, scale=-1.0).then_inc(mt_copied, 1)
                    act.wait_ge(mt_copied, c * GROUPS + g + 1)
                    q = qs[g % GROUPS]
                    for r in range(2):
                        act.dma_start(q[ROWS_MAX + r:ROWS_MAX + r + 1, :, :].bitcast(F32),
                                      mt[4 * r:4 * r + 4, :].bitcast(F32)).then_inc(m_loaded[g % GROUPS], 16)

                copy_maxima(0, 0)

                def item(c, name, g, i, more):
                    if name == "loc":
                        act.wait_ge(loc_scored, c * 20 + 5 * g + i + 1)
                        if i == 0:
                            at_least(act, pvl_done, GROUPS, c, g)
                        nc.scalar.activation(p_loc[:, i, :, :], ps_loc[:].rearrange("p b (j n) -> p (b j) n", j=2)[:, :, WIN:256],
                                             ACT.Exp, scale=SCALE).then_inc(loc_exped, 1)
                    if name == "last":
                        act.wait_ge(loc_scored, c * 20 + 5 * g + 5)
                        nc.scalar.activation(p_last[P - WIN:P, :, :],
                                             ps_loc[P - WIN:P].rearrange("p b (j n) -> p (b j) n", j=2)[:, :, 256 - WIN:256],
                                             ACT.Exp, scale=SCALE).then_inc(loc_exped, 1)
                    if name == "glob":
                        act.wait_ge(glob_scored, c * 16 + 4 * g + i + 1)
                        if i == 0:
                            at_least(act, pvg_done, GROUPS, c, g)
                        nc.scalar.activation(p_glob[:, i, :], ps_glob[:], ACT.Exp, scale=SCALE).then_inc(glob_exped, 1)
                    if name == "mt":
                        copy_maxima(c, g + 1)
                    if name == "pvl":
                        act.wait_ge(pvl_done, c * GROUPS + g + 1)
                        invert(c, 2 * g + 1)
                    if name == "pvg":
                        act.wait_ge(pvg_done, c * GROUPS + g)
                        invert(c, 2 * g)
                    if name == "ot":
                        act.wait_ge(o_sum, c * GROUPS + g)
                        at_least(act, out_mm, TILES, c, 0 if g else -TILES)
                        nc.scalar.activation(ot_hi[:, (g - 1) % GROUPS, :], o_loc[:], ACT.Copy, scale=-1.0).then_inc(oth_done, 1)
                    if name == "tr":
                        act.wait_ge(tr_done, c * TILES + i + 1 - TILES)
                        at_least(act, ffn_mm, TILES, c, max(i - 1, 0) - TILES)
                        nc.scalar.activation(th[:, i % 2, :, :].rearrange("p k n -> p (k n)"), ps_misc[:], ACT.Copy).then_inc(th_done, 1)

                chunks(act, item)

            @block.vector
            def _(dve):
                nc.vector.memset(one_row, 1.0).then_inc(const_made, 1)
                for g in range(GROUPS):
                    nc.vector.memset(qs[g][3 * DH:ROWS_EXP, :, :].bitcast(F32), 1.0).then_inc(const_made, 1)
                    nc.vector.memset(ks[g][3 * DH:ROWS_EXP, :, :].bitcast(F32), 0.0).then_inc(const_made, 1)
                    nc.vector.memset(kgs[g][3 * DH:ROWS_EXP, :, :].bitcast(F32), 0.0).then_inc(const_made, 1)

                def maxima(c, g, u):
                    i, pair = u % TILES, u // TILES
                    dve.wait_ge(max_scored, c * 32 + 8 * g + u + 1)
                    if u == 0:
                        at_least(dve, mt_done, GROUPS, c, g - 1)
                    off = WIN if i == TILES - 1 else 0
                    dst = mx[g % 2][:, i, :, 2 * pair:2 * pair + 2]
                    nc.vector.tensor_reduce(dst[:, 0, :], ps_max[:, :, off:off + MW], axis=AX.X, op=ALU.max)
                    goff = 256 + (0 if pair == 0 else P)
                    nc.vector.tensor_reduce(dst[:, 1, :], ps_max[:, :, goff:goff + NGLOB], axis=AX.X, op=ALU.max).then_inc(max_taken, 1)

                for u in range(8):
                    maxima(0, 0, u)
                dve.wait_ge(const_loaded, CONST_LOADS)

                def normalise(c, off, dst):
                    dve.wait_ge(inv_done, c * 8 + off)
                    nc.vector.tensor_tensor(rtmp[:], ps_s[:], rinv[:], ALU.mult).then_inc(nr_step, 1)
                    dve.wait_ge(nr_step, c * 16 + 2 * off - 1)
                    nc.vector.scalar_tensor_tensor(out=rtmp[:], in0=rtmp[:], scalar=-2.0, in1=rinv[:],
                                                   op0=ALU.add, op1=ALU.mult).then_inc(nr_step, 1)
                    dve.wait_ge(nr_step, c * 16 + 2 * off)
                    nc.vector.tensor_tensor(dst[:], ps_o[:], rtmp[:], ALU.mult).then_inc(o_done, 1)

                def layer_stats(c, s, i, src):
                    n = c * TILES + i + 1 - TILES
                    nc.vector.bn_stats(bn[s][:, i, :], src).then_inc(bn_done[s], 1)
                    dve.wait_ge(bn_done[s], n)
                    dve.sem_inc(held, 1)
                    nc.vector.bn_aggr(mv[s][:, i, :], bn[s][:, i, :]).then_inc(aggr_done[s], 1)

                def layer_norm(c, s, i, dst, src):
                    n = c * TILES + i + 1 - TILES
                    dve.wait_ge(rs_done[s], n)
                    dve.wait_ge(aggr_done[s], n)
                    nc.vector.tensor_scalar(dst, src, mv[s][:, i, 0:1], rs[s][:, i:i + 1],
                                            ALU.subtract, ALU.mult).then_inc(nm_done[s], 1)

                def item(c, name, g, i, more):
                    n = c * TILES + i + 1 - TILES
                    if name == "max":
                        maxima(c, g + 1, i)
                    if name == "pvl":
                        at_least(dve, otl_done, GROUPS, c, g)
                        normalise(c, 2 * g + 1, o_loc)
                    if name == "pvg":
                        normalise(c, 2 * g, o_glob)
                    if name == "ot":
                        dve.wait_ge(oth_done, c * GROUPS + g)
                        nc.vector.scalar_tensor_tensor(out=ot_lo[:, (g - 1) % GROUPS, :], in0=o_loc[:], scalar=-1.0,
                                                       in1=ot_hi[:, (g - 1) % GROUPS, :].bitcast(F32),
                                                       op0=ALU.mult, op1=ALU.subtract).then_inc(otl_done, 1)
                    if name == "out":
                        dve.wait_ge(out_mm, n)
                        at_least(dve, y_stored[i], 16, c, -16)
                        nc.vector.tensor_tensor(yb[:, i, :], ps_misc[:], bo[:], ALU.add).then_inc(y_added, 1)
                        dve.wait_ge(y_added, n)
                        layer_stats(c, 0, i, yb[:, i, :])
                    if name == "y":
                        layer_norm(c, 0, i, yb[:, i, :], yb[:, i, :])
                    if name == "x1":
                        dve.wait_ge(x1_done, n)
                        layer_stats(c, 1, i, xb[:, i, :])
                    if name == "x1n":
                        layer_norm(c, 1, i, yb[:, i, :], xb[:, i, :])
                    if name == "tr":
                        dve.wait_ge(th_done, n)
                        nc.vector.tensor_tensor(tl[:, i % 2, :, :].rearrange("p k n -> p (k n)"), ps_misc[:],
                                                th[:, i % 2, :, :].rearrange("p k n -> p (k n)").bitcast(F32),
                                                ALU.subtract).then_inc(tl_done, 1)
                    if name == "ffn":
                        dve.wait_ge(ffn_mm, n)
                        nc.vector.tensor_tensor(yb[:, i, :], ps_misc[:], bf[:], ALU.add).then_inc(z_added, 1)
                        dve.wait_ge(z_added, n)
                        layer_stats(c, 2, i, yb[:, i, :])
                    if name == "z":
                        layer_norm(c, 2, i, yb[:, i, :], yb[:, i, :])

                chunks(dve, item)

            @block.tensor
            def _(pe):
                pe.wait_ge(const_loaded, CONST_LOADS)
                pe.wait_ge(mask_cast, 16)
                pe.wait_ge(ident_cast, 16)
                pe.wait_ge(const_made, CONST_MADE)

                def score_maxima(c, g, u):
                    i, pair = u % TILES, u // TILES
                    if u == 0:
                        pe.wait_ge(st_loaded[g % GROUPS], c * 160 + 160 * (g // GROUPS + 1))
                    at_least(pe, max_taken, 32, c, 8 * g + u)
                    w0, off = (SPAN - 256, WIN) if i == TILES - 1 else (i * P, 0)
                    q, k, kg = qs[g % GROUPS], ks[g % GROUPS], kgs[g % GROUPS]
                    for b in range(2):
                        h = 2 * pair + b
                        hg = h if pair == 0 else h - 1
                        lhs = q[0:ROWS_MAX, h, i * P:(i + 1) * P]
                        nc.tensor.matmul(ps_max[:, b, 0:256], lhs, k[0:ROWS_MAX, h, w0:w0 + 256], start=True, stop=False)
                        nc.tensor.matmul(ps_max[:, b, off:off + MW], ident_b[:], mask[:, 0:MW], start=False, stop=True)
                        last = nc.tensor.matmul(ps_max[:, b, 256:512], lhs,
                                                kg[0:ROWS_MAX, hg:hg + 2, :], start=True, stop=True)
                    last.then_inc(max_scored, 1)

                def misc_free(c, prev):
                    name, g, i = prev
                    if name == "mt":
                        at_least(pe, mt_copied, GROUPS, c, g + 2)
                    if name == "out":
                        pe.wait_ge(y_added, c * TILES + i + 1 - TILES)
                    if name == "tr":
                        pe.wait_ge(tl_done, c * TILES + i + 1 - TILES)
                    if name == "ffn":
                        pe.wait_ge(z_added, c * TILES + i + 1 - TILES)

                def transpose_maxima(c, g):
                    pe.wait_ge(max_taken, c * 32 + 8 * g + 8)
                    for i in range(TILES):
                        last = nc.tensor.transpose(ps_misc[0:8, i * P:(i + 1) * P],
                                                   mx[g % 2][:, i, :, :].rearrange("p a h -> p (a h)"), ident[:])
                    last.then_inc(mt_done, 1)

                for u in range(8):
                    score_maxima(0, 0, u)
                transpose_maxima(0, 0)

                MASK = MW
                prev_of = {}

                def item(c, name, g, i, more):
                    if isinstance(c, int):
                        prev_of.update(misc_users(c < NCHUNK, c > 0, more))
                    elif name == "loc" and g == 0 and i == 0:
                        prev_of.update(misc_users(True, True, True))
                    if name == "loc":
                        if i == 0:
                            pe.wait_ge(m_loaded[g], c * 32 + 32)
                        at_least(pe, loc_exped, 20, c, 5 * g + i)
                        for b in range(2):
                            nc.tensor.matmul(ps_loc[:, b, :], ident_b[:], mask[:, MASK + b * 512:MASK + (b + 1) * 512], start=True, stop=False)
                            for jj in range(2):
                                j = 2 * b + jj
                                if j == 0:
                                    rhs = qs[g][0:ROWS_EXP, i:i + 1, 0:P].to_broadcast([ROWS_EXP, 2, P])
                                else:
                                    x0 = (0, 0, P, 2 * P)[j]
                                    rhs = qs[g][0:ROWS_EXP, i, x0:x0 + 256]
                                last = nc.tensor.matmul(ps_loc[:, b, jj * 256:(jj + 1) * 256], ks[g][0:ROWS_EXP, i, j * P:(j + 1) * P],
                                                        rhs, start=False, stop=jj == 1)
                        last.then_inc(loc_scored, 1)
                    if name == "last":
                        at_least(pe, loc_exped, 20, c, 5 * g + 4)
                        for b in range(2):
                            nc.tensor.matmul(ps_loc[:, b, :], ident_b[:], mask[:, MASK + 1024:MASK + 1536], start=True, stop=False)
                            for jj in range(2):
                                last = nc.tensor.matmul(ps_loc[:, b, jj * 256:(jj + 1) * 256],
                                                        ks[g][0:ROWS_EXP, 2 * b + jj, SPAN - P:SPAN],
                                                        qs[g][0:ROWS_EXP, 2 * b + jj, CHUNK - 256:CHUNK], start=False, stop=jj == 1)
                        last.then_inc(loc_scored, 1)
                    if name == "glob":
                        at_least(pe, glob_exped, 16, c, 4 * g + i)
                        nc.tensor.matmul(ps_glob[:], kgs[g][0:ROWS_EXP, i, :], qs[g][0:ROWS_EXP, i, :],
                                         start=True, stop=True).then_inc(glob_scored, 1)
                    if name == "max":
                        score_maxima(c, g + 1, i)
                    if name == "mt":
                        misc_free(c, prev_of[name, g, i])
                        transpose_maxima(c, g + 1)
                    if name == "pvl":
                        pe.wait_ge(loc_exped, c * 20 + 5 * g + 5)
                        pe.wait_ge(v_loaded[g], c * 48 + 48)
                        at_least(pe, o_done, 8, c, 2 * g)
                        for j in range(5):
                            for dst, vals in ((ps_o, None), (ps_s, ones)):
                                for h in range(4):
                                    if j < 4:
                                        lhs = vw[g][:, j, h * DH:(h + 1) * DH] if vals is None else ones[:]
                                        x0, w = (0, P) if j == 0 else (WIN + P * (j - 1), MW)
                                        rhs = p_loc[:, h, j, MW - w:MW]
                                    else:
                                        lhs = vl[g][P - WIN:P, h * DH:(h + 1) * DH] if vals is None else ones[P - WIN:P, :]
                                        x0, w = CHUNK - WIN, WIN
                                        rhs = p_last[P - WIN:P, h, :]
                                    last = nc.tensor.matmul(dst[h * DH:(h + 1) * DH, x0:x0 + w], lhs, rhs,
                                                            start=j == 0, stop=j == 4, skip_group_check=True)
                        last.then_inc(pvl_done, 1)
                    if name == "pvg":
                        gp = (g - 1) % GROUPS
                        pe.wait_ge(glob_exped, c * 16 + 4 * g)
                        at_least(pe, o_done, 8, c, 2 * g - 1)
                        for dst, vals in ((ps_o, None), (ps_s, ones)):
                            for h in range(4):
                                lhs = vg[gp][:, h * DH:(h + 1) * DH] if vals is None else ones[:]
                                last = nc.tensor.matmul(dst[h * DH:(h + 1) * DH, :], lhs, p_glob[:, h, :], start=True, stop=True)
                        last.then_inc(pvg_done, 1)
                    if name in ("out", "ffn"):
                        misc_free(c, prev_of[name, g, i])
                        if name == "out":
                            pe.wait_ge(otl_done, c * GROUPS)
                            a_hi, a_lo, w_hi, w_lo = ot_hi, ot_lo, wo_hi, wo_lo
                            cols = slice(i * P, (i + 1) * P)
                            pick = lambda t, k: t[:, k, cols]
                        else:
                            pe.wait_ge(tl_done, c * TILES + i + 1 - TILES)
                            a_hi, a_lo, w_hi, w_lo = th, tl, m_hi, m_lo
                            pick = lambda t, k: t[:, i % 2, k, :]
                        for k in range(KT):
                            for n, (a, w) in enumerate(((a_hi, w_hi), (a_lo, w_hi), (a_hi, w_lo))):
                                last = nc.tensor.matmul(ps_misc[:], pick(a, k), w[:, k, :], start=k == 0 and n == 0,
                                                        stop=k == KT - 1 and n == 2)
                        last.then_inc(out_mm if name == "out" else ffn_mm, 1)
                    if name == "tr":
                        misc_free(c, prev_of[name, g, i])
                        pe.wait_ge(nm_done[1], c * TILES + i + 1 - TILES)
                        for k in range(KT):
                            last = nc.tensor.transpose(ps_misc[:, k * P:(k + 1) * P], yb[:, i, k * P:(k + 1) * P], ident[:])
                        last.then_inc(tr_done, 1)

                chunks(pe, item)


def build(nc, x, w_qkv, w_out, b_out, w_real, w_imag, b_ffn, dft_d, mask_d, ident_d, out):
    dram = lambda n, shape: nc.dram_tensor(n, shape, F32, kind="Internal").ap()
    q_hi_d, q_lo_d = dram("q_hi_d", (D, TOK)), dram("q_lo_d", (D, TOK))
    k_hi_d, k_lo_d = dram("k_hi_d", (D, BATCH * PSEQ)), dram("k_lo_d", (D, BATCH * PSEQ))
    v_d = dram("v_d", (BATCH * PSEQ, D))
    kg_hi_d, kg_lo_d = dram("kg_hi_d", (D, BATCH * NGLOB)), dram("kg_lo_d", (D, BATCH * NGLOB))
    bias_d = dram("bias_d", (1, BATCH * PSEQ))
    project_phase(nc, x, w_qkv, q_hi_d, q_lo_d, k_hi_d, k_lo_d, v_d, kg_hi_d, kg_lo_d, bias_d, ident_d)
    with ExitStack() as ctx:
        m_hi, m_lo, wo_hi, wo_lo = (ctx.enter_context(nc.sbuf_tensor(n, [P, KT, D], F32R))
                                    for n in ("m_hi", "m_lo", "wo_hi", "wo_lo"))
        spectral_phase(nc, w_real, w_imag, dft_d, w_out, m_hi, m_lo, wo_hi, wo_lo)
        attention_phase(nc, x, b_out, b_ffn, q_hi_d, q_lo_d, k_hi_d, k_lo_d, v_d, kg_hi_d, kg_lo_d, bias_d,
                        ident_d, mask_d, m_hi, m_lo, wo_hi, wo_lo, out)


_INS = ['L0_attn_x', 'L0_attn_w_qkv', 'L0_attn_w_out', 'L0_attn_b_out', 'L0_ffn_w_freq_real', 'L0_ffn_w_freq_imag', 'L0_ffn_bias']


def kernel(**inputs):
    import concourse.bacc as bacc
    from concourse.bass_utils import run_bass_kernel_spmd as run

    nc = bacc.Bacc("TRN2", target_bir_lowering=False, num_devices=1)
    arrays, args = {}, []
    given = {n: np.ascontiguousarray(inputs[n]) for n in _INS}
    given |= {"dft": dft(), "masks": masks(), "identity": np.eye(P, dtype=np.float32)}
    for name, a in given.items():
        arrays[f"in_{name}"] = a
        args.append(nc.dram_tensor(f"in_{name}", a.shape, mybir.dt.from_np(a.dtype), kind="ExternalInput").ap())
    args.append(nc.dram_tensor("out_0", (BATCH, SEQ, D), F32, kind="ExternalOutput").ap())
    build(nc, *args)
    r = run(nc, [arrays], core_ids=[0])
    return r.results[0]["out_0"]
```

```python
import numpy as np
import concourse.bass as bass
from concourse import mybir
from contextlib import ExitStack

F32 = mybir.dt.float32
F32R = mybir.dt.float32r
BF16 = mybir.dt.bfloat16
ACT = mybir.ActivationFunctionType
ALU = mybir.AluOpType
AX = mybir.AxisListType

P = 128
BATCH, SEQ, D = 2, 8192, 512
HEADS, WIN = 16, 64
DH = D // HEADS
SCALE = float(DH) ** -0.5
HALF = WIN // 2
TOK = BATCH * SEQ
KT = D // P
CHUNK = 512
NCHUNK = TOK // CHUNK
CPB = SEQ // CHUNK
TILES = CHUNK // P
SPAN = CHUNK + 2 * HALF
PSEQ = SEQ + 2 * HALF
NGLOB = SEQ // WIN
GROUPS = HEADS // 4
ROWS_MAX = 3 * DH + 1
ROWS_EXP = 3 * DH + 3
NEG = -1e30
EPS = 1e-5


def masks():
    def banned(key, query):
        ok = (key - query >= 0) & (key - query <= WIN - 1)
        return np.where(ok, 0.0, NEG).astype(np.float32)
    part = np.arange(P)[:, None]
    m_max = banned(np.arange(P + WIN)[None, :], part)
    x = np.arange(256)[None, :]
    m_first = banned(part, x % P)
    m_first[:, :P] = NEG
    m_one = banned(P + part, x)
    m_mid = banned(2 * P + part, P + x)
    m_last = banned(CHUNK - HALF * 2 + part, 256 + x)
    return np.concatenate([m_max, m_first, m_one, m_mid, m_mid, m_last, m_last], axis=1)


def dft():
    n = np.arange(D)
    angle = 2.0 * np.pi * ((n[:, None] * n[None, :]) % D) / D
    c, s = np.cos(angle), np.sin(angle)
    return np.stack([c, s, c / D, -s / D]).astype(np.float32)


def project_phase(nc, x, w_qkv, q_hi_d, q_lo_d, k_hi_d, k_lo_d, v_d, kg_hi_d, kg_lo_d, bias_d, ident_d):
    NOUT = 2 * KT
    with ExitStack() as ctx:
        sb = lambda n, s, d: ctx.enter_context(nc.sbuf_tensor(n, s, d))
        sem = lambda n: ctx.enter_context(nc.semaphore(n))
        w_hi = sb("w_hi", [P, KT, 3 * D], F32R)
        w_lo = sb("w_lo", [P, KT, 3 * D], F32R)
        w_raw = sb("w_raw", [P, 2, D], F32)
        xb = [sb(f"xb{u}", [P, TILES, D], F32) for u in range(2)]
        ht_hi = [sb(f"ht_hi{u}", [P, KT, CHUNK], F32R) for u in range(2)]
        ht_lo = [sb(f"ht_lo{u}", [P, KT, CHUNK], F32R) for u in range(2)]
        o_hi = [sb(f"o_hi{u}", [P, NOUT, CHUNK], F32R) for u in range(2)]
        o_lo = [sb(f"o_lo{u}", [P, NOUT, CHUNK], F32R) for u in range(2)]
        o_v = [sb(f"o_v{u}", [P, TILES, D], F32) for u in range(2)]
        kg_hi = sb("kg_hi", [P, KT, BATCH * NGLOB], F32R)
        kg_lo = sb("kg_lo", [P, KT, BATCH * NGLOB], F32R)
        ident = sb("ident_a", [P, P], F32)
        bn = [sb(f"bn{u}", [P, TILES, 6], F32) for u in range(2)]
        mv = [sb(f"mv{u}", [P, TILES, 2], F32) for u in range(2)]
        ve = [sb(f"ve{u}", [P, TILES], F32) for u in range(2)]
        rstd = [sb(f"rstd{u}", [P, TILES], F32) for u in range(2)]
        mhalf = sb("mhalf_a", [P, TILES], F32)
        pt = [ctx.enter_context(nc.psum_tensor(f"pt{i}", [P, KT, P], F32)) for i in range(2)]
        po = [ctx.enter_context(nc.psum_tensor(f"po{i}", [P, D], F32)) for i in range(6)]
        zero = sb("zero", [P, D], F32)
        negs = sb("negs", [1, HALF], F32)

        raw_loaded = [sem(f"raw_loaded{i}") for i in range(2)]
        w_hi_done, w_lo_done = sem("w_hi_done"), sem("w_lo_done")
        ident_loaded = sem("ident_loaded")
        x_loaded = [sem(f"x_loaded{u}") for u in range(2)]
        inited = sem("inited")
        held = sem("held")
        bn_done, aggr_done = sem("bn_done"), sem("aggr_done")
        ve_done, rstd_done = sem("ve_done"), sem("rstd_done")
        xn_done = sem("xn_done")
        t_done, t_hi, t_lo = sem("t_done"), sem("t_hi"), sem("t_lo")
        mm_done, ev_act, ev_dve = sem("mm_done"), sem("ev_act"), sem("ev_dve")
        stored = [sem(f"stored{u}") for u in range(2)]
        kg_copied, kg_stored, pads = sem("kg_copied"), sem("kg_stored"), sem("pads")

        x_v = x.rearrange("b (n p) d -> p (b n) d", p=P)

        def at_least(eng, s, per, c, off):
            if not isinstance(c, int) or per * c + off > 0:
                eng.wait_ge(s, c * per + off)

        def chunks(eng, body, first):
            first()
            for c in range(2):
                body(c, c, 2)
            with eng.Fori(1, NCHUNK // 2 - 1) as pair:
                for u in range(2):
                    body(pair * 2 + u, u, 2)
            body(NCHUNK - 2, 0, 1)
            body(NCHUNK - 1, 1, 0)

        with nc.Block() as block:
            @block.sync
            def _(sp):
                for n in range(3 * KT):
                    if n >= 2:
                        sp.wait_ge(w_hi_done, n - 1)
                        sp.wait_ge(w_lo_done, n - 1)
                    if n == 1:
                        sp.dma_start(ident[:], ident_d).then_inc(ident_loaded, 16)
                    if n == 2:
                        for u in range(2):
                            sp.dma_start(xb[u][:], x_v[:, u * TILES:(u + 1) * TILES, :]).then_inc(x_loaded[u], 16)
                    kt, part = n // 3, n % 3
                    sp.dma_start(w_raw[:, n % 2, :],
                                 w_qkv[kt * P:(kt + 1) * P, part * D:(part + 1) * D]).then_inc(raw_loaded[n % 2], 16)
                sp.wait_ge(inited, 3)
                n_pads = 0
                for b in range(BATCH):
                    for at in (b * PSEQ, b * PSEQ + HALF + SEQ):
                        for kd in (k_hi_d, k_lo_d):
                            sp.dma_start(kd[:, at:at + HALF].rearrange("(a p) n -> p a n", p=P),
                                         zero[:, 0:KT * HALF].rearrange("p (a n) -> p a n", a=KT)).then_inc(pads, 16)
                        sp.dma_start(v_d[at:at + HALF, :], zero[0:HALF, :]).then_inc(pads, 16)
                        sp.dma_start(bias_d[:, at:at + HALF], negs[:, :]).then_inc(pads, 16)
                        n_pads += 4
                    sp.dma_start(bias_d[:, b * PSEQ + HALF:b * PSEQ + HALF + SEQ].rearrange("o (p n) -> (o p) n", p=P),
                                 zero[:, 0:SEQ // P]).then_inc(pads, 16)
                    n_pads += 1

                def body(c, u, follow):
                    if follow == 2:
                        sp.wait_ge(t_done, c * TILES + TILES)
                        sp.dma_start(xb[u][:], x_v[:, bass.ds((c + 2) * TILES, TILES), :]).then_inc(x_loaded[u], 16)
                    sp.wait_ge(ev_act, c * (NOUT + TILES) + NOUT + TILES)
                    sp.wait_ge(ev_dve, c * NOUT + NOUT)
                    pad_at = c * CHUNK + (c // CPB) * (PSEQ - SEQ) + HALF
                    for src, qd, kd in ((o_hi[u], q_hi_d, k_hi_d), (o_lo[u], q_lo_d, k_lo_d)):
                        sp.dma_start(qd.rearrange("(a p) n -> p a n", p=P)[:, :, bass.ds(c * CHUNK, CHUNK)],
                                     src[:, 0:KT, :].bitcast(F32)).then_inc(stored[u], 16)
                        sp.dma_start(kd.rearrange("(a p) n -> p a n", p=P)[:, :, bass.ds(pad_at, CHUNK)],
                                     src[:, KT:NOUT, :].bitcast(F32)).then_inc(stored[u], 16)
                    sp.dma_start(v_d[bass.ds(pad_at, CHUNK), :].rearrange("(t p) d -> p t d", p=P),
                                 o_v[u][:]).then_inc(stored[u], 16)

                chunks(sp, body, lambda: None)
                sp.wait_ge(kg_copied, 2 * NCHUNK)
                sp.dma_start(kg_hi_d.rearrange("(a p) n -> p a n", p=P), kg_hi[:].bitcast(F32)).then_inc(kg_stored, 16)
                sp.dma_start(kg_lo_d.rearrange("(a p) n -> p a n", p=P), kg_lo[:].bitcast(F32)).then_inc(kg_stored, 16)
                sp.wait_ge(kg_stored, 32)
                sp.wait_ge(pads, 16 * n_pads)
                for u in range(2):
                    sp.wait_ge(stored[u], 16 * 5 * NCHUNK // 2)

            @block.gpsimd
            def _(pool):
                pool.memset(zero[:], 0.0).then_inc(inited, 1)
                pool.memset(negs[:], NEG).then_inc(inited, 1)
                pool.memset(mhalf[:], -0.5).then_inc(inited, 1)
                pool.wait_ge(inited, 3)

                def rstds(c, u):
                    pool.wait_ge(aggr_done, c * TILES + TILES)
                    pool.sem_inc(held, 1)
                    pool.tensor_scalar(ve[u][:], mv[u][:, :, 1], EPS, None, ALU.add).then_inc(ve_done, 1)
                    pool.wait_ge(ve_done, c + 1)
                    pool.tensor_tensor(rstd[u][:], ve[u][:], mhalf[:], ALU.pow).then_inc(rstd_done, 1)

                def body(c, u, follow):
                    pool.wait_ge(ev_act, c * (NOUT + TILES) + NOUT)
                    pool.wait_ge(ev_dve, c * NOUT + NOUT)
                    for src, dst in ((o_hi[u], kg_hi), (o_lo[u], kg_lo)):
                        pool.tensor_copy(dst[:, :, bass.ds(c * (CHUNK // WIN), CHUNK // WIN)],
                                         src[:, KT:NOUT, ::WIN].bitcast(F32)).then_inc(kg_copied, 1)
                    if follow == 2:
                        rstds(c + 2, u)

                chunks(pool, body, lambda: [rstds(u, u) for u in range(2)])

            @block.scalar
            def _(act):
                for n in range(3 * KT):
                    kt, part = n // 3, n % 3
                    act.wait_ge(raw_loaded[n % 2], 16 * (n // 2 + 1))
                    nc.scalar.activation(w_hi[:, kt, part * D:(part + 1) * D], w_raw[:, n % 2, :], ACT.Copy).then_inc(w_hi_done, 1)

                def t_evac(c, u, t):
                    act.wait_ge(t_done, c * TILES + t + 1)
                    if t == 0:
                        at_least(act, mm_done, NOUT + TILES, c, -(NOUT + TILES))
                    nc.scalar.activation(ht_hi[u][:, :, t * P:(t + 1) * P], pt[t % 2][:], ACT.Copy).then_inc(t_hi, 1)

                def body(c, u, follow):
                    if not isinstance(c, int) or c >= 2:
                        act.wait_ge(stored[u], (c // 2) * 80)
                        act.wait_ge(kg_copied, c * 2 - 2)
                    for o in range(NOUT + TILES):
                        act.wait_ge(mm_done, c * (NOUT + TILES) + o + 1)
                        dst = o_hi[u][:, o, :] if o < NOUT else o_v[u][:, o - NOUT, :]
                        nc.scalar.activation(dst, po[o % 6][:], ACT.Copy).then_inc(ev_act, 1)
                        if follow and o % 3 == 2:
                            t_evac(c + 1, 1 - u, o // 3)

                chunks(act, body, lambda: [t_evac(0, 0, t) for t in range(TILES)])

            @block.vector
            def _(dve):
                for n in range(3 * KT):
                    kt, part = n // 3, n % 3
                    dve.wait_ge(w_hi_done, n + 1)
                    nc.vector.tensor_tensor(w_lo[:, kt, part * D:(part + 1) * D], w_raw[:, n % 2, :],
                                            w_hi[:, kt, part * D:(part + 1) * D].bitcast(F32), ALU.subtract).then_inc(w_lo_done, 1)

                def stats(c, u, t):
                    if t == 0:
                        dve.wait_ge(x_loaded[u], (c // 2) * 16 + 16)
                    nc.vector.bn_stats(bn[u][:, t, :], xb[u][:, t, :]).then_inc(bn_done, 1)
                    dve.wait_ge(bn_done, c * TILES + t + 1)
                    dve.sem_inc(held, 1)
                    nc.vector.bn_aggr(mv[u][:, t, :], bn[u][:, t, :]).then_inc(aggr_done, 1)

                def norm(c, u, t):
                    if t == 0:
                        dve.wait_ge(rstd_done, c + 1)
                        dve.wait_ge(aggr_done, c * TILES + TILES)
                    nc.vector.tensor_scalar(xb[u][:, t, :], xb[u][:, t, :], mv[u][:, t, 0:1], rstd[u][:, t:t + 1],
                                            ALU.subtract, ALU.mult).then_inc(xn_done, 1)

                def t_evac(c, u, t):
                    dve.wait_ge(t_hi, c * TILES + t + 1)
                    if t == 0:
                        at_least(dve, mm_done, NOUT + TILES, c, -(NOUT + TILES))
                    nc.vector.tensor_tensor(ht_lo[u][:, :, t * P:(t + 1) * P], pt[t % 2][:],
                                            ht_hi[u][:, :, t * P:(t + 1) * P].bitcast(F32), ALU.subtract).then_inc(t_lo, 1)

                def first():
                    for u in range(2):
                        for t in range(TILES):
                            stats(u, u, t)
                    for t in range(TILES):
                        norm(0, 0, t)
                    for t in range(TILES):
                        t_evac(0, 0, t)

                def body(c, u, follow):
                    if follow:
                        for t in range(TILES):
                            norm(c + 1, 1 - u, t)
                    if not isinstance(c, int) or c >= 2:
                        dve.wait_ge(stored[u], (c // 2) * 80)
                        dve.wait_ge(kg_copied, c * 2 - 2)
                    for o in range(NOUT + TILES):
                        if o < NOUT:
                            dve.wait_ge(ev_act, c * (NOUT + TILES) + o + 1)
                            nc.vector.tensor_tensor(o_lo[u][:, o, :], po[o % 6][:], o_hi[u][:, o, :].bitcast(F32),
                                                    ALU.subtract).then_inc(ev_dve, 1)
                        if follow == 2 and o >= NOUT:
                            stats(c + 2, u, o - NOUT)
                        if follow and o % 3 == 2:
                            t_evac(c + 1, 1 - u, o // 3)

                chunks(dve, body, first)

            @block.tensor
            def _(pe):
                pe.wait_ge(ident_loaded, 16)

                def transposes(c, u, t):
                    pe.wait_ge(xn_done, c * TILES + t + 1)
                    at_least(pe, t_lo, TILES, c, t - 1)
                    for k in range(KT):
                        last = nc.tensor.transpose(pt[t % 2][:, k, :], xb[u][:, t, k * P:(k + 1) * P], ident[:])
                    last.then_inc(t_done, 1)

                def body(c, u, follow):
                    pe.wait_ge(t_hi, c * TILES + TILES)
                    pe.wait_ge(t_lo, c * TILES + TILES)
                    for o in range(NOUT + TILES):
                        p = (o - 6) % (NOUT + TILES)
                        off = 0 if o >= 6 else -1
                        if p < NOUT:
                            at_least(pe, ev_dve, NOUT, c, off * NOUT + p + 1)
                        else:
                            at_least(pe, ev_act, NOUT + TILES, c, off * (NOUT + TILES) + p + 1)
                        for k in range(KT):
                            for n, (ha, wa) in enumerate(((ht_hi, w_hi), (ht_lo, w_hi), (ht_hi, w_lo))):
                                start, stop = k == 0 and n == 0, k == KT - 1 and n == 2
                                if o < NOUT:
                                    last = nc.tensor.matmul(po[o % 6][:], wa[:, k, o * P:(o + 1) * P], ha[u][:, k, :],
                                                            start=start, stop=stop)
                                else:
                                    t = o - NOUT
                                    last = nc.tensor.matmul(po[o % 6][:], ha[u][:, k, t * P:(t + 1) * P],
                                                            wa[:, k, 2 * D:3 * D], start=start, stop=stop)
                        last.then_inc(mm_done, 1)
                        if follow and o % 3 == 1:
                            transposes(c + 1, 1 - u, o // 3)

                def first():
                    for t in range(TILES):
                        transposes(0, 0, t)
                    pe.wait_ge(w_lo_done, 3 * KT)

                chunks(pe, body, first)


def spectral_phase(nc, w_real, w_imag, dft_d, w_out, m_hi, m_lo, wo_hi, wo_lo):
    with ExitStack() as ctx:
        sb = lambda n, s, d: ctx.enter_context(nc.sbuf_tensor(n, s, d))
        sem = lambda n: ctx.enter_context(nc.semaphore(n))
        wr, wi, wo = (sb(n, [P, KT, D], F32) for n in ("wr", "wi", "wo_raw"))
        tr = [sb(f"dft{i}", [P, KT, D], F32) for i in range(4)]
        nwr = sb("nwr", [P, KT, D], F32)
        at, bt = sb("at", [P, KT, D], F32), sb("bt", [P, KT, D], F32)
        ps = [ctx.enter_context(nc.psum_tensor(f"pm{i}", [P, D], F32)) for i in range(4)]
        first_loaded, loaded, neg_done, mm_done, ab_done = sem("s_first"), sem("s_loaded"), sem("s_neg"), sem("s_mm"), sem("s_ab")
        hi_done, lo_done = sem("s_hi"), sem("s_lo")
        with nc.Block() as block:
            @block.sync
            def _(sp):
                rows = lambda src: src.rearrange("(a p) n -> p a n", p=P)
                for src, dst in ((w_real, wr), (dft_d[0], tr[0]), (w_imag, wi), (dft_d[1], tr[1])):
                    sp.dma_start(dst[:], rows(src)).then_inc(first_loaded, 16)
                for src, dst in ((dft_d[2], tr[2]), (dft_d[3], tr[3]), (w_out, wo)):
                    sp.dma_start(dst[:], rows(src)).then_inc(loaded, 16)

            @block.tensor
            def _(pe):
                pe.wait_ge(first_loaded, 16 * 4)
                pe.wait_ge(neg_done, 1)
                steps = [(wr, tr[0], wi, tr[1]), (wi, tr[0], nwr, tr[1]), (at, tr[2], bt, tr[3])]
                n = 0
                for l0, r0, l1, r1 in steps:
                    if l0 is at:
                        pe.wait_ge(loaded, 16 * 3)
                        pe.wait_ge(ab_done, 2 * KT)
                    for a in range(KT):
                        if 4 <= n < 2 * KT:
                            pe.wait_ge(ab_done, n - 3)
                        for k in range(KT):
                            nc.tensor.matmul(ps[n % 4][:], l0[:, k, a * P:(a + 1) * P], r0[:, k, :], start=k == 0, stop=False)
                            last = nc.tensor.matmul(ps[n % 4][:], l1[:, k, a * P:(a + 1) * P], r1[:, k, :], start=False, stop=k == KT - 1)
                        last.then_inc(mm_done, 1)
                        n += 1

            @block.scalar
            def _(act):
                act.wait_ge(loaded, 16 * 3)
                for k in range(KT):
                    nc.scalar.activation(wo_hi[:, k, :], wo[:, k, :], ACT.Copy).then_inc(hi_done, 1)
                for a in range(KT):
                    act.wait_ge(mm_done, 2 * KT + a + 1)
                    nc.scalar.activation(m_hi[:, a, :], ps[a][:], ACT.Copy).then_inc(hi_done, 1)

            @block.vector
            def _(dve):
                dve.wait_ge(first_loaded, 16 * 4)
                nc.vector.tensor_scalar(nwr[:], wr[:], -1.0, None, ALU.mult).then_inc(neg_done, 1)
                for n in range(2 * KT):
                    dve.wait_ge(mm_done, n + 1)
                    nc.vector.tensor_copy((at if n < KT else bt)[:, n % KT, :], ps[n % 4][:]).then_inc(ab_done, 1)
                for k in range(KT):
                    dve.wait_ge(hi_done, k + 1)
                    nc.vector.tensor_tensor(wo_lo[:, k, :], wo[:, k, :], wo_hi[:, k, :].bitcast(F32), ALU.subtract).then_inc(lo_done, 1)
                for a in range(KT):
                    dve.wait_ge(hi_done, KT + a + 1)
                    nc.vector.tensor_tensor(m_lo[:, a, :], ps[a][:], m_hi[:, a, :].bitcast(F32), ALU.subtract).then_inc(lo_done, 1)


def attention_phase(nc, x, b_out, b_ffn, q_hi_d, q_lo_d, k_hi_d, k_lo_d, v_d, kg_hi_d, kg_lo_d, bias_d,
                    ident_d, mask_d, m_hi, m_lo, wo_hi, wo_lo, out):
    with ExitStack() as ctx:
        sb = lambda n, s, d: ctx.enter_context(nc.sbuf_tensor(n, s, d))
        pb = lambda n, s: ctx.enter_context(nc.psum_tensor(n, s, F32))
        sem = lambda n: ctx.enter_context(nc.semaphore(n))
        MW = P + WIN
        qs = [sb(f"qs{g}", [P, 4, CHUNK], F32R) for g in range(GROUPS)]
        ks = [sb(f"ks{g}", [P, 4, SPAN], F32R) for g in range(GROUPS)]
        kgs = [sb(f"kgs{g}", [P, 4, NGLOB], F32R) for g in range(GROUPS)]
        vw = [sb(f"vw{g}", [P, 4, P], F32) for g in range(GROUPS)]
        vl = [sb(f"vl{g}", [P, P], F32) for g in range(GROUPS)]
        vg = [sb(f"vg{g}", [P, P], F32) for g in range(GROUPS)]
        p_loc = sb("p_loc", [P, 4, 4, MW], F32)
        p_last = sb("p_last", [P, 4, WIN], F32)
        p_glob = sb("p_glob", [P, 4, CHUNK], F32)
        ones = sb("ones", [P, DH], F32)
        mask = sb("mask", [P, MW + 6 * 256], BF16)
        ident = sb("ident", [P, P], F32)
        ident_b = sb("ident_b", [P, P], BF16)
        one_row = p_loc[0:1, 0, 0:3, :].rearrange("p j n -> p (j n)")
        CONST_MADE = 3 + 3 * GROUPS
        CONST_LOADS = 16 * (3 + 2 * GROUPS)
        mx = [sb(f"mx{u}", [P, TILES, 2, 4], F32) for u in range(2)]
        mt = sb("mt", [8, CHUNK], F32R)
        s_sb, lns, rinv, rtmp = (sb(n, [P, CHUNK], F32) for n in ("s_sb", "lns", "rinv", "rtmp"))
        o_loc = sb("o_loc", [P, CHUNK], F32)
        o_glob = sb("o_glob", [P, CHUNK], F32)
        ot_hi = sb("ot_hi", [P, KT, CHUNK], F32R)
        ot_lo = sb("ot_lo", [P, KT, CHUNK], F32R)
        xb = sb("x_res", [P, TILES, D], F32)
        yb = sb("y_buf", [P, TILES, D], F32)
        th = sb("th", [P, 2, KT, P], F32R)
        tl = sb("tl", [P, 2, KT, P], F32R)
        bo = sb("bo", [P, D], F32)
        bf = sb("bf", [P, D], F32)
        bn = [sb(f"bnb{s}", [P, TILES, 6], F32) for s in range(3)]
        mv = [sb(f"mvb{s}", [P, TILES, 2], F32) for s in range(3)]
        ve = [sb(f"veb{s}", [P, TILES], F32) for s in range(3)]
        rs = [sb(f"rsb{s}", [P, TILES], F32) for s in range(3)]
        mhalf = sb("mhalf_b", [P, 1], F32)

        ps_max = [pb(f"ps_max{b}", [P, 512]) for b in range(2)]
        ps_loc = pb("ps_loc", [P, 2, 512])
        ps_glob = pb("ps_glob", [P, 512])
        ps_misc = pb("ps_misc", [P, 512])
        ps_o = pb("ps_o", [P, 512])
        ps_s = pb("ps_s", [P, 512])

        held = sem("held_b")
        mask_cast, ident_cast = sem("mask_cast"), sem("ident_cast")
        const_loaded, const_made = sem("const_loaded"), sem("const_made")
        st_loaded = [sem(f"st_loaded{g}") for g in range(GROUPS)]
        v_loaded = [sem(f"v_loaded{g}") for g in range(GROUPS)]
        m_loaded = [sem(f"m_loaded{g}") for g in range(GROUPS)]
        x_loaded = [sem(f"xr_loaded{i}") for i in range(TILES)]
        y_stored = [sem(f"y_stored{i}") for i in range(TILES)]
        max_scored, max_taken = sem("max_scored"), sem("max_taken")
        mt_done, mt_copied = sem("mt_done"), sem("mt_copied")
        loc_scored, loc_exped = sem("loc_scored"), sem("loc_exped")
        glob_scored, glob_exped = sem("glob_scored"), sem("glob_exped")
        pvl_done, pvg_done = sem("pvl_done"), sem("pvg_done")
        o_copied, s_copied = sem("o_copied"), sem("s_copied")
        ln_done, inv_done = sem("ln_done"), sem("inv_done")
        nr_step = sem("nr_step")
        o_done = sem("o_done")
        o_sum = sem("o_sum")
        oth_done, otl_done = sem("oth_done"), sem("otl_done")
        out_mm, ffn_mm, tr_done = sem("out_mm"), sem("ffn_mm"), sem("tr_done")
        y_added, z_added = sem("y_added"), sem("z_added")
        th_done, tl_done = sem("th_done"), sem("tl_done")
        bn_done = [sem(f"bnb_done{s}") for s in range(3)]
        aggr_done = [sem(f"aggrb_done{s}") for s in range(3)]
        ve_done = [sem(f"veb_done{s}") for s in range(3)]
        rs_done = [sem(f"rsb_done{s}") for s in range(3)]
        nm_done = [sem(f"nmb_done{s}") for s in range(3)]
        x1_done, z_done = sem("x1_done"), sem("z_done")

        def at_least(eng, s, per, c, off):
            if not isinstance(c, int) or per * c + off > 0:
                eng.wait_ge(s, c * per + off)

        TAIL_AT = dict(z=(36, 44, 52, 61), x1=(22, 25, 28, 31), y=(20, 23, 26, 29), x1n=(25, 33, 41, 49),
                       outa=(17, 20, 23, 26), outs=(18, 21, 24, 27), ffna=(33, 41, 49, 58), ffns=(34, 42, 50, 59),
                       trl=(30, 37, 45, 53), out=(16, 19, 22, 25), tr=(28, 35, 43, 51), ffn=(32, 40, 48, 57))
        STEP = {2: [("pvlc", 0)], 3: [("nl", 0), ("loc", 0)], 4: [("pvg", 0)], 5: [("pvg", 1)],
                6: [("nl", 1), ("loc", 1)], 7: [("nl", 2)], 8: [("glob", 0), ("pvgc", 0)], 9: [("ng", 0), ("loc", 2)],
                10: [("glob", 1)], 11: [("ng", 1)], 12: [("ng", 2), ("last", 3)], 13: [("glob", 2)],
                14: [("loc", 3)], 15: [("ot", 0)],
                16: [("otl", 0), ("glob", 3), ("pvl", 0), ("mt", 0), ("pvl", 1), ("pvl", 2), ("pvl", 3), ("pvl", 4)]}
        OF_BEFORE = ("pvlc", "nl", "pvg", "pvgc", "ng", "ot", "otl")

        def order(attend, tail, more):
            items = []
            for g in range(GROUPS):
                ahead = attend and (more or g < GROUPS - 1)
                for k in range(17):
                    for name, i in STEP.get(k, ()):
                        if name in OF_BEFORE:
                            if (attend and g > 0) or (g == 0 and tail):
                                items.append((name, g, i))
                        elif ahead if name == "mt" else attend:
                            items.append((name, g, i))
                    if ahead and k < 16:
                        items.append(("max", g, k))
                    if tail and k < 16:
                        items += [(name, g, at.index(16 * g + k)) for name, at in TAIL_AT.items() if 16 * g + k in at]
            return items

        def chunks(eng, item):
            for c, kind in ((0, "first"), (None, "loop"), (NCHUNK - 1, "final"), (NCHUNK, "tail")):
                attend, tail, more = kind != "tail", kind != "first", kind in ("first", "loop")
                if kind == "loop":
                    with eng.Fori(1, NCHUNK - 1) as cc:
                        for it in order(attend, tail, more):
                            item(cc, *it, more)
                else:
                    for it in order(attend, tail, more):
                        item(c, *it, more)

        def misc_users(attend, tail, more):
            users = [("mt", GROUPS - 1, 0)] + [it for it in order(attend, tail, more)
                                               if it[0] in ("mt", "out", "tr", "ffn")]
            return dict(zip(users[1:], [("mt", -1 if attend else -2, 0)] + users[1:-1]))

        with nc.Block() as block:
            @block.sync
            def _(sp):
                sp.dma_start(ident[:], ident_d).then_inc(const_loaded, 16)
                sp.dma_start(bo[:], b_out.rearrange("(o n) -> o n", o=1).to_broadcast([P, D])).then_inc(const_loaded, 16)
                sp.dma_start(bf[:], b_ffn.rearrange("(o n) -> o n", o=1).to_broadcast([P, D])).then_inc(const_loaded, 16)

                def load_stack(c, g):
                    pad_at = c * CHUNK + (c // CPB) * (PSEQ - SEQ)
                    glob_at = (c // CPB) * NGLOB
                    rows = slice(g * P, (g + 1) * P)
                    for r, (qd, kd, gd) in enumerate(((q_hi_d, k_hi_d, kg_hi_d), (q_hi_d, k_lo_d, kg_lo_d),
                                                      (q_lo_d, k_hi_d, kg_hi_d))):
                        dst = slice(r * DH, (r + 1) * DH)
                        sp.dma_start(qs[g][dst, :, :].bitcast(F32),
                                     qd[rows, :].rearrange("(h p) n -> p h n", p=DH)[:, :, bass.ds(c * CHUNK, CHUNK)]).then_inc(st_loaded[g], 16)
                        sp.dma_start(ks[g][dst, :, :].bitcast(F32),
                                     kd[rows, :].rearrange("(h p) n -> p h n", p=DH)[:, :, bass.ds(pad_at, SPAN)]).then_inc(st_loaded[g], 16)
                        sp.dma_start(kgs[g][dst, :, :].bitcast(F32),
                                     gd[rows, :].rearrange("(h p) n -> p h n", p=DH)[:, :, bass.ds(glob_at, NGLOB)]).then_inc(st_loaded[g], 16)
                    sp.dma_start(ks[g][3 * DH:ROWS_MAX, :, :].bitcast(F32),
                                 bias_d[:, bass.ds(pad_at, SPAN)].rearrange("o (a n) -> o a n", a=1).to_broadcast([1, 4, SPAN])).then_inc(st_loaded[g], 16)

                def load_values(c, g):
                    pad_at = c * CHUNK + (c // CPB) * (PSEQ - SEQ)
                    cols = slice(g * P, (g + 1) * P)
                    sp.dma_start(vw[g][:], v_d[bass.ds(pad_at, CHUNK), cols].rearrange("(t p) d -> p t d", p=P)).then_inc(v_loaded[g], 16)
                    sp.dma_start(vl[g][P - WIN:P, :], v_d[bass.ds(pad_at + CHUNK, WIN), cols]).then_inc(v_loaded[g], 16)
                    sp.dma_start(vg[g][:], v_d[bass.ds((c // CPB) * PSEQ + HALF, SEQ), cols]
                                 .rearrange("(t w) d -> t w d", w=WIN)[:, 0, :]).then_inc(v_loaded[g], 16)

                sp.wait_ge(const_made, CONST_MADE)
                for i in range(TILES):
                    sp.sem_inc(y_stored[i], 16)
                for g in range(GROUPS):
                    load_stack(0, g)
                    load_values(0, g)

                def item(c, name, g, i, more):
                    if name == "loc" and g == 0 and i == 0:
                        if not isinstance(c, int) or c > 0:
                            for t in range(TILES):
                                    sp.dma_start(xb[:, t, :], x.rearrange("b n d -> (b n) d")[bass.ds((c - 1) * CHUNK + t * P, P), :]).then_inc(x_loaded[t], 16)
                    if name == "pvgc":
                        sp.wait_ge(pvg_done, c * GROUPS + g)
                        if g > 0 and more:
                            load_values(c + 1, g - 1)
                        if g == 0 and (not isinstance(c, int) or c < NCHUNK):
                            load_values(c, GROUPS - 1)
                    if name == "glob" and i == 3 and more:
                        sp.wait_ge(glob_scored, c * 16 + 4 * g + 4)
                        load_stack(c + 1, g)
                    if name == "z":
                        n = c * TILES + i + 1 - TILES
                        sp.wait_ge(z_done, n)
                        sp.dma_start(out.rearrange("b n d -> (b n) d")[bass.ds((c - 1) * CHUNK + i * P, P), :],
                                     yb[:, i, :]).then_inc(y_stored[i], 16)

                for c, kind in ((0, "first"), (None, "loop"), (NCHUNK - 1, "final"), (NCHUNK, "tail")):
                    if kind == "loop":
                        with sp.Fori(1, NCHUNK - 1) as cc:
                            for it in order(True, True, True):
                                item(cc, *it, True)
                    else:
                        if kind == "tail":
                            item(c, "loc", 0, 0, False)
                        for it in order(kind != "tail", kind != "first", kind == "first"):
                            item(c, *it, kind == "first")
                for i in range(TILES):
                    sp.wait_ge(y_stored[i], 16 * (NCHUNK + 1))

            @block.gpsimd
            def _(pool):
                pool.memset(ones[:], 1.0).then_inc(const_made, 1)
                pool.memset(mhalf[:], -0.5).then_inc(const_made, 1)
                pool.dma_start(mask[:], mask_d).then_inc(mask_cast, 16)
                pool.dma_start(ident_b[:], ident_d).then_inc(ident_cast, 16)
                pool.wait_ge(const_made, 2)

                def power(c, s, i):
                    n = c * TILES + i + 1 - TILES
                    pool.wait_ge(aggr_done[s], n)
                    pool.sem_inc(held, 1)
                    pool.tensor_scalar(ve[s][:, i:i + 1], mv[s][:, i, 1:2], EPS, None, ALU.add).then_inc(ve_done[s], 1)
                    pool.wait_ge(ve_done[s], n)
                    pool.tensor_tensor(rs[s][:, i:i + 1], ve[s][:, i:i + 1], mhalf[:], ALU.pow).then_inc(rs_done[s], 1)

                def item(c, name, g, i, more):
                    n = c * TILES + i + 1 - TILES
                    if name == "outs":
                        power(c, 0, i)
                    if name == "y":
                        pool.wait_ge(nm_done[0], n)
                        pool.wait_ge(x_loaded[i], c * 16)
                        pool.tensor_tensor(xb[:, i, :], xb[:, i, :], yb[:, i, :], ALU.add).then_inc(x1_done, 1)
                    if name == "x1":
                        power(c, 1, i)
                    if name == "ffns":
                        power(c, 2, i)
                    if name == "z":
                        pool.wait_ge(nm_done[2], n)
                        pool.tensor_tensor(yb[:, i, :], yb[:, i, :], xb[:, i, :], ALU.add).then_inc(z_done, 1)
                    if (name, i) in (("nl", 0), ("ng", 0)):
                        off = 2 * g - 1 if name == "nl" else 2 * g
                        pool.wait_ge(inv_done, c * 8 + off)
                        pool.tensor_tensor(rtmp[:], s_sb[:], rinv[:], ALU.mult).then_inc(nr_step, 1)
                    if name == "ng" and i == 2:
                        pool.wait_ge(nr_step, c * 16 + 4 * g)
                        pool.tensor_tensor(o_glob[:], o_glob[:], rtmp[:], ALU.mult).then_inc(o_done, 1)
                        pool.wait_ge(o_done, (c * GROUPS + g) * 2)
                        at_least(pool, otl_done, GROUPS, c, g - 1)
                        pool.tensor_tensor(o_loc[:], o_loc[:], o_glob[:], ALU.add).then_inc(o_sum, 1)

                chunks(pool, item)

            @block.scalar
            def _(act):
                nc.scalar.preload_act_table_set("natural_log_exp_and_others")
                act.wait_ge(const_made, CONST_MADE)
                for g in range(GROUPS):
                    act.dma_start(ks[g][ROWS_MAX:ROWS_MAX + 1, :, :].bitcast(F32),
                                  one_row.rearrange("o (a n) -> o a n", a=1).to_broadcast([1, 4, SPAN])).then_inc(const_loaded, 16)
                    act.dma_start(kgs[g][ROWS_MAX + 1:ROWS_EXP, :, :].bitcast(F32),
                                  one_row[:, 0:4 * NGLOB]).then_inc(const_loaded, 16)

                def invert(c, off):
                    at_least(act, o_done, 8, c, off - 1)
                    nc.scalar.activation(s_sb[:], ps_s[:], ACT.Copy).then_inc(s_copied, 1)
                    act.wait_ge(s_copied, c * 8 + off)
                    nc.scalar.activation(lns[:], s_sb[:], ACT.Ln).then_inc(ln_done, 1)
                    act.wait_ge(ln_done, c * 8 + off)
                    nc.scalar.activation(rinv[:], lns[:], ACT.Exp, scale=-1.0).then_inc(inv_done, 1)

                def copy_maxima(c, g):
                    act.wait_ge(mt_done, c * GROUPS + g + 1)
                    if g > 0:
                        act.wait_ge(m_loaded[g - 1], c * 32 + 32)
                    nc.scalar.activation(mt[:], ps_misc[0:8, :], ACT.Copy, scale=-1.0).then_inc(mt_copied, 1)
                    act.wait_ge(mt_copied, c * GROUPS + g + 1)
                    q = qs[g % GROUPS]
                    for r in range(2):
                        act.dma_start(q[ROWS_MAX + r:ROWS_MAX + r + 1, :, :].bitcast(F32),
                                      mt[4 * r:4 * r + 4, :].bitcast(F32)).then_inc(m_loaded[g % GROUPS], 16)

                copy_maxima(0, 0)

                def item(c, name, g, i, more):
                    if name == "loc":
                        act.wait_ge(loc_scored, c * 20 + 5 * g + (i if i < 3 else 4) + 1)
                        if i == 0:
                            at_least(act, pvl_done, GROUPS, c, g)
                        nc.scalar.activation(p_loc[:, i, :, :], ps_loc[:].rearrange("p b (j n) -> p (b j) n", j=2)[:, :, WIN:256],
                                             ACT.Exp, scale=SCALE).then_inc(loc_exped, 1)
                    if name == "last":
                        act.wait_ge(loc_scored, c * 20 + 5 * g + 4)
                        nc.scalar.activation(p_last[P - WIN:P, :, :],
                                             ps_loc[P - WIN:P].rearrange("p b (j n) -> p (b j) n", j=2)[:, :, 256 - WIN:256],
                                             ACT.Exp, scale=SCALE).then_inc(loc_exped, 1)
                    if name == "glob":
                        act.wait_ge(glob_scored, c * 16 + 4 * g + i + 1)
                        if i == 0:
                            at_least(act, pvg_done, GROUPS, c, g)
                        nc.scalar.activation(p_glob[:, i, :], ps_glob[:], ACT.Exp, scale=SCALE).then_inc(glob_exped, 1)
                    if name == "mt":
                        copy_maxima(c, g + 1)
                    if name == "pvl" and i == 4:
                        act.wait_ge(pvl_done, c * GROUPS + g + 1)
                        invert(c, 2 * g + 1)
                    if name == "pvgc":
                        act.wait_ge(pvg_done, c * GROUPS + g)
                        invert(c, 2 * g)
                    if name == "ot":
                        act.wait_ge(o_sum, c * GROUPS + g)
                        if g > 0:
                            at_least(act, out_mm, TILES, c, 0)
                        nc.scalar.activation(ot_hi[:, (g - 1) % GROUPS, :], o_loc[:], ACT.Copy, scale=-1.0).then_inc(oth_done, 1)
                    if name == "tr":
                        act.wait_ge(tr_done, c * TILES + i + 1 - TILES)
                        nc.scalar.activation(th[:, i % 2, :, :].rearrange("p k n -> p (k n)"), ps_misc[:], ACT.Copy).then_inc(th_done, 1)

                chunks(act, item)

            @block.vector
            def _(dve):
                nc.vector.memset(one_row, 1.0).then_inc(const_made, 1)
                for g in range(GROUPS):
                    nc.vector.memset(qs[g][3 * DH:ROWS_EXP, :, :].bitcast(F32), 1.0).then_inc(const_made, 1)
                    nc.vector.memset(ks[g][3 * DH:ROWS_EXP, :, :].bitcast(F32), 0.0).then_inc(const_made, 1)
                    nc.vector.memset(kgs[g][3 * DH:ROWS_EXP, :, :].bitcast(F32), 0.0).then_inc(const_made, 1)

                def maxima(c, g, k):
                    i, pair, b = k // 2 % TILES, k // (2 * TILES), k % 2
                    if k == 0:
                        at_least(dve, mt_done, GROUPS, c, g - 1)
                    off = WIN if i == TILES - 1 else 0
                    goff = 256 + (0 if pair == 0 else P)
                    h = 2 * pair + b
                    dve.wait_ge(max_scored, c * 64 + 16 * g + k + 1)
                    nc.vector.tensor_reduce(mx[g % 2][:, i, 0, h:h + 1], ps_max[b][:, off:off + MW], axis=AX.X, op=ALU.max)
                    nc.vector.tensor_reduce(mx[g % 2][:, i, 1, h:h + 1], ps_max[b][:, goff:goff + NGLOB], axis=AX.X, op=ALU.max).then_inc(max_taken, 1)

                for k in range(16):
                    maxima(0, 0, k)
                dve.wait_ge(const_loaded, CONST_LOADS)

                def newton(c, off):
                    dve.wait_ge(nr_step, c * 16 + 2 * off - 1)
                    nc.vector.scalar_tensor_tensor(out=rtmp[:], in0=rtmp[:], scalar=-2.0, in1=rinv[:],
                                                   op0=ALU.add, op1=ALU.mult).then_inc(nr_step, 1)

                def layer_stats(c, s, i, src):
                    n = c * TILES + i + 1 - TILES
                    nc.vector.bn_stats(bn[s][:, i, :], src).then_inc(bn_done[s], 1)
                    dve.wait_ge(bn_done[s], n)
                    dve.sem_inc(held, 1)
                    nc.vector.bn_aggr(mv[s][:, i, :], bn[s][:, i, :]).then_inc(aggr_done[s], 1)

                def layer_norm(c, s, i, dst, src):
                    n = c * TILES + i + 1 - TILES
                    dve.wait_ge(rs_done[s], n)
                    dve.wait_ge(aggr_done[s], n)
                    nc.vector.tensor_scalar(dst, src, mv[s][:, i, 0:1], rs[s][:, i:i + 1],
                                            ALU.subtract, ALU.mult).then_inc(nm_done[s], 1)

                def item(c, name, g, i, more):
                    n = c * TILES + i + 1 - TILES
                    if name == "max":
                        maxima(c, g + 1, i)
                    if name == "pvlc":
                        dve.wait_ge(pvl_done, c * GROUPS + g)
                        at_least(dve, otl_done, GROUPS, c, g - 1)
                        nc.vector.tensor_copy(o_loc[:], ps_o[:]).then_inc(o_copied, 1)
                    if name == "pvgc":
                        dve.wait_ge(pvg_done, c * GROUPS + g)
                        at_least(dve, o_sum, GROUPS, c, g - 1)
                        nc.vector.tensor_copy(o_glob[:], ps_o[:]).then_inc(o_copied, 1)
                    if name == "nl" and i == 1:
                        newton(c, 2 * g - 1)
                    if name == "nl" and i == 2:
                        dve.wait_ge(nr_step, c * 16 + 4 * g - 2)
                        nc.vector.tensor_tensor(o_loc[:], o_loc[:], rtmp[:], ALU.mult).then_inc(o_done, 1)
                    if name == "ng" and i == 1:
                        newton(c, 2 * g)
                    if name == "otl":
                        dve.wait_ge(oth_done, c * GROUPS + g)
                        nc.vector.scalar_tensor_tensor(out=ot_lo[:, (g - 1) % GROUPS, :], in0=o_loc[:], scalar=-1.0,
                                                       in1=ot_hi[:, (g - 1) % GROUPS, :].bitcast(F32),
                                                       op0=ALU.mult, op1=ALU.subtract).then_inc(otl_done, 1)
                    if name == "outa":
                        dve.wait_ge(out_mm, n)
                        dve.wait_ge(y_stored[i], c * 16)
                        nc.vector.tensor_tensor(yb[:, i, :], ps_misc[:], bo[:], ALU.add).then_inc(y_added, 1)
                    if name == "outs":
                        dve.wait_ge(y_added, n)
                        layer_stats(c, 0, i, yb[:, i, :])
                    if name == "y":
                        layer_norm(c, 0, i, yb[:, i, :], yb[:, i, :])
                    if name == "x1":
                        dve.wait_ge(x1_done, n)
                        layer_stats(c, 1, i, xb[:, i, :])
                    if name == "x1n":
                        layer_norm(c, 1, i, yb[:, i, :], xb[:, i, :])
                    if name == "trl":
                        dve.wait_ge(th_done, n)
                        nc.vector.tensor_tensor(tl[:, i % 2, :, :].rearrange("p k n -> p (k n)"), ps_misc[:],
                                                th[:, i % 2, :, :].rearrange("p k n -> p (k n)").bitcast(F32),
                                                ALU.subtract).then_inc(tl_done, 1)
                    if name == "ffna":
                        dve.wait_ge(ffn_mm, n)
                        nc.vector.tensor_tensor(yb[:, i, :], ps_misc[:], bf[:], ALU.add).then_inc(z_added, 1)
                    if name == "ffns":
                        dve.wait_ge(z_added, n)
                        layer_stats(c, 2, i, yb[:, i, :])
                    if name == "z":
                        layer_norm(c, 2, i, yb[:, i, :], yb[:, i, :])

                chunks(dve, item)

            @block.tensor
            def _(pe):
                pe.wait_ge(const_loaded, CONST_LOADS)
                pe.wait_ge(mask_cast, 16)
                pe.wait_ge(ident_cast, 16)
                pe.wait_ge(const_made, CONST_MADE)

                def score_maxima(c, g, k):
                    i, pair, b = k // 2 % TILES, k // (2 * TILES), k % 2
                    if k == 0:
                        pe.wait_ge(st_loaded[g % GROUPS], c * 160 + 160 * (g // GROUPS + 1))
                    w0, off = (SPAN - 256, WIN) if i == TILES - 1 else (i * P, 0)
                    h = 2 * pair + b
                    hg = h if pair == 0 else h - 1
                    at_least(pe, max_taken, 64, c, 16 * g + k - 1)
                    lhs = qs[g % GROUPS][0:ROWS_MAX, h, i * P:(i + 1) * P]
                    nc.tensor.matmul(ps_max[b][:, 0:256], lhs, ks[g % GROUPS][0:ROWS_MAX, h, w0:w0 + 256], start=True, stop=False)
                    nc.tensor.matmul(ps_max[b][:, off:off + MW], ident_b[:], mask[:, 0:MW], start=False, stop=True)
                    nc.tensor.matmul(ps_max[b][:, 256:512], lhs,
                                     kgs[g % GROUPS][0:ROWS_MAX, hg:hg + 2, :], start=True, stop=True).then_inc(max_scored, 1)

                def misc_free(c, prev):
                    name, g, i = prev
                    if name == "mt":
                        at_least(pe, mt_copied, GROUPS, c, g + 2)
                    if name == "out":
                        pe.wait_ge(y_added, c * TILES + i + 1 - TILES)
                    if name == "tr":
                        pe.wait_ge(tl_done, c * TILES + i + 1 - TILES)
                    if name == "ffn":
                        pe.wait_ge(z_added, c * TILES + i + 1 - TILES)

                def transpose_maxima(c, g):
                    pe.wait_ge(max_taken, c * 64 + 16 * g + 16)
                    for i in range(TILES):
                        last = nc.tensor.transpose(ps_misc[0:8, i * P:(i + 1) * P],
                                                   mx[g % 2][:, i, :, :].rearrange("p a h -> p (a h)"), ident[:])
                    last.then_inc(mt_done, 1)

                for k in range(16):
                    score_maxima(0, 0, k)
                transpose_maxima(0, 0)

                MASK = MW
                prev_of = {}

                def item(c, name, g, i, more):
                    if isinstance(c, int):
                        prev_of.update(misc_users(c < NCHUNK, c > 0, more))
                    elif name == "loc" and g == 0 and i == 0:
                        prev_of.update(misc_users(True, True, True))
                    if name == "loc":
                        if i == 0:
                            pe.wait_ge(m_loaded[g], c * 32 + 32)
                        at_least(pe, loc_exped, 20, c, 5 * g + (i if i < 3 else 4))
                        for b in range(2):
                            nc.tensor.matmul(ps_loc[:, b, :], ident_b[:], mask[:, MASK + b * 512:MASK + (b + 1) * 512], start=True, stop=False)
                            for jj in range(2):
                                j = 2 * b + jj
                                if j == 0:
                                    rhs = qs[g][0:ROWS_EXP, i:i + 1, 0:P].to_broadcast([ROWS_EXP, 2, P])
                                else:
                                    x0 = (0, 0, P, 2 * P)[j]
                                    rhs = qs[g][0:ROWS_EXP, i, x0:x0 + 256]
                                last = nc.tensor.matmul(ps_loc[:, b, jj * 256:(jj + 1) * 256], ks[g][0:ROWS_EXP, i, j * P:(j + 1) * P],
                                                        rhs, start=False, stop=jj == 1)
                        last.then_inc(loc_scored, 1)
                    if name == "last":
                        at_least(pe, loc_exped, 20, c, 5 * g + 3)
                        for b in range(2):
                            nc.tensor.matmul(ps_loc[:, b, :], ident_b[:], mask[:, MASK + 1024:MASK + 1536], start=True, stop=False)
                            for jj in range(2):
                                last = nc.tensor.matmul(ps_loc[:, b, jj * 256:(jj + 1) * 256],
                                                        ks[g][0:ROWS_EXP, 2 * b + jj, SPAN - P:SPAN],
                                                        qs[g][0:ROWS_EXP, 2 * b + jj, CHUNK - 256:CHUNK], start=False, stop=jj == 1)
                        last.then_inc(loc_scored, 1)
                    if name == "glob":
                        at_least(pe, glob_exped, 16, c, 4 * g + i)
                        nc.tensor.matmul(ps_glob[:], kgs[g][0:ROWS_EXP, i, :], qs[g][0:ROWS_EXP, i, :],
                                         start=True, stop=True).then_inc(glob_scored, 1)
                    if name == "max":
                        score_maxima(c, g + 1, i)
                    if name == "mt":
                        misc_free(c, prev_of[name, g, i])
                        transpose_maxima(c, g + 1)
                    if name == "pvl":
                        if i == 0:
                            pe.wait_ge(loc_exped, c * 20 + 5 * g + 5)
                            pe.wait_ge(v_loaded[g], c * 48 + 48)
                            at_least(pe, o_copied, 8, c, 2 * g)
                            at_least(pe, s_copied, 8, c, 2 * g)
                        for j in (i,):
                            for dst, vals in ((ps_o, None), (ps_s, ones)):
                                for h in range(4):
                                    if j < 4:
                                        lhs = vw[g][:, j, h * DH:(h + 1) * DH] if vals is None else ones[:]
                                        x0, w = (0, P) if j == 0 else (WIN + P * (j - 1), MW)
                                        rhs = p_loc[:, h, j, MW - w:MW]
                                    else:
                                        lhs = vl[g][P - WIN:P, h * DH:(h + 1) * DH] if vals is None else ones[P - WIN:P, :]
                                        x0, w = CHUNK - WIN, WIN
                                        rhs = p_last[P - WIN:P, h, :]
                                    last = nc.tensor.matmul(dst[h * DH:(h + 1) * DH, x0:x0 + w], lhs, rhs,
                                                            start=j == 0, stop=j == 4, skip_group_check=True)
                        if i == 4:
                            last.then_inc(pvl_done, 1)
                    if name == "pvg":
                        gp = (g - 1) % GROUPS
                        if i == 0:
                            pe.wait_ge(glob_exped, c * 16 + 4 * g)
                            at_least(pe, o_copied, 8, c, 2 * g - 1)
                        else:
                            at_least(pe, s_copied, 8, c, 2 * g - 1)
                        for h in range(4):
                            lhs = vg[gp][:, h * DH:(h + 1) * DH] if i == 0 else ones[:]
                            last = nc.tensor.matmul((ps_o, ps_s)[i][h * DH:(h + 1) * DH, :], lhs, p_glob[:, h, :], start=True, stop=True)
                        if i == 1:
                            last.then_inc(pvg_done, 1)
                    if name in ("out", "ffn"):
                        misc_free(c, prev_of[name, g, i])
                        if name == "out":
                            pe.wait_ge(otl_done, c * GROUPS)
                            a_hi, a_lo, w_hi, w_lo = ot_hi, ot_lo, wo_hi, wo_lo
                            cols = slice(i * P, (i + 1) * P)
                            pick = lambda t, k: t[:, k, cols]
                        else:
                            pe.wait_ge(tl_done, c * TILES + i + 1 - TILES)
                            a_hi, a_lo, w_hi, w_lo = th, tl, m_hi, m_lo
                            pick = lambda t, k: t[:, i % 2, k, :]
                        for k in range(KT):
                            for n, (a, w) in enumerate(((a_hi, w_hi), (a_lo, w_hi), (a_hi, w_lo))):
                                last = nc.tensor.matmul(ps_misc[:], pick(a, k), w[:, k, :], start=k == 0 and n == 0,
                                                        stop=k == KT - 1 and n == 2)
                        last.then_inc(out_mm if name == "out" else ffn_mm, 1)
                    if name == "tr":
                        misc_free(c, prev_of[name, g, i])
                        pe.wait_ge(nm_done[1], c * TILES + i + 1 - TILES)
                        for k in range(KT):
                            last = nc.tensor.transpose(ps_misc[:, k * P:(k + 1) * P], yb[:, i, k * P:(k + 1) * P], ident[:])
                        last.then_inc(tr_done, 1)

                chunks(pe, item)


def build(nc, x, w_qkv, w_out, b_out, w_real, w_imag, b_ffn, dft_d, mask_d, ident_d, out):
    dram = lambda n, shape: nc.dram_tensor(n, shape, F32, kind="Internal").ap()
    q_hi_d, q_lo_d = dram("q_hi_d", (D, TOK)), dram("q_lo_d", (D, TOK))
    k_hi_d, k_lo_d = dram("k_hi_d", (D, BATCH * PSEQ)), dram("k_lo_d", (D, BATCH * PSEQ))
    v_d = dram("v_d", (BATCH * PSEQ, D))
    kg_hi_d, kg_lo_d = dram("kg_hi_d", (D, BATCH * NGLOB)), dram("kg_lo_d", (D, BATCH * NGLOB))
    bias_d = dram("bias_d", (1, BATCH * PSEQ))
    project_phase(nc, x, w_qkv, q_hi_d, q_lo_d, k_hi_d, k_lo_d, v_d, kg_hi_d, kg_lo_d, bias_d, ident_d)
    with ExitStack() as ctx:
        m_hi, m_lo, wo_hi, wo_lo = (ctx.enter_context(nc.sbuf_tensor(n, [P, KT, D], F32R))
                                    for n in ("m_hi", "m_lo", "wo_hi", "wo_lo"))
        spectral_phase(nc, w_real, w_imag, dft_d, w_out, m_hi, m_lo, wo_hi, wo_lo)
        attention_phase(nc, x, b_out, b_ffn, q_hi_d, q_lo_d, k_hi_d, k_lo_d, v_d, kg_hi_d, kg_lo_d, bias_d,
                        ident_d, mask_d, m_hi, m_lo, wo_hi, wo_lo, out)


_INS = ['L0_attn_x', 'L0_attn_w_qkv', 'L0_attn_w_out', 'L0_attn_b_out', 'L0_ffn_w_freq_real', 'L0_ffn_w_freq_imag', 'L0_ffn_bias']


def kernel(**inputs):
    import concourse.bacc as bacc
    from concourse.bass_utils import run_bass_kernel_spmd as run

    nc = bacc.Bacc("TRN2", target_bir_lowering=False, num_devices=1)
    arrays, args = {}, []
    given = {n: np.ascontiguousarray(inputs[n]) for n in _INS}
    given |= {"dft": dft(), "masks": masks(), "identity": np.eye(P, dtype=np.float32)}
    for name, a in given.items():
        arrays[f"in_{name}"] = a
        args.append(nc.dram_tensor(f"in_{name}", a.shape, mybir.dt.from_np(a.dtype), kind="ExternalInput").ap())
    args.append(nc.dram_tensor("out_0", (BATCH, SEQ, D), F32, kind="ExternalOutput").ap())
    build(nc, *args)
    r = run(nc, [arrays], core_ids=[0])
    return r.results[0]["out_0"]
```
